# Optimizing a Trainium2 kernel written in Bass

```python
import numpy as np
import jax
import jax.numpy as jnp

def _softmax(x, axis=-1):
    return jax.nn.softmax(x, axis=axis)
def _gelu(x):
    return jax.nn.gelu(x, approximate=True)
def _silu(x):
    return jax.nn.silu(x)
def _sigmoid(x):
    return jax.nn.sigmoid(x)
def _layernorm(x, axis=-1, eps=1e-5):
    m = jnp.mean(x, axis=axis, keepdims=True)
    v = jnp.var(x, axis=axis, keepdims=True)
    return (x - m) / jnp.sqrt(v + eps)
def _scatter_add(tgt, idx, src, axis=0):
    return tgt.at[idx].add(src)
def _segment_sum(src, seg, n):
    return jax.ops.segment_sum(src, seg, n)

kernel_name = 'mk_conv_preact_d2_conv_nchw192_1a3352'

def setup_inputs(seed: int = 0):
    np.random.seed(seed)
    _w = jnp.asarray
    def _rec_inputs():
        import jax
        import jax.numpy as jnp
        _gk = jax.random.key(seed)
        x = -0.000357 + 1 * jax.random.normal(jax.random.fold_in(_gk, 1), (32, 192, 56, 56), jnp.float32)
        return x
    x = _rec_inputs()
    def _L0_conv_setup():
        import jax, jax.numpy as jnp
        import numpy as np
        HEADS, HEAD_DIM = (8, 32)
        FOLD_H, FOLD_W = (2, 2)
        PH, PW = (2, 2)
        EPS = 1e-12

        def conv1x1(x, W, b):
            return jnp.einsum('bchw,oc->bohw', x, W) + b[None, :, None, None]
        key = jax.random.key(seed)
        ks = jax.random.split(key, 4)
        B, Cin, H, Wd = (32, 192, 56, 56)
        Cout = 192
        D = HEADS * HEAD_DIM

        def winit(k, shape, fan_in):
            return jax.random.normal(k, shape, jnp.float32) * (1.0 / np.sqrt(fan_in))
        return {'x': jax.random.normal(ks[0], (B, Cin, H, Wd), jnp.float32), 'W1': winit(ks[1], (D, Cin), Cin), 'b1': jnp.zeros((D,), jnp.float32), 'Wv': winit(ks[2], (D, Cin), Cin), 'bv': jnp.zeros((D,), jnp.float32), 'W2': winit(ks[3], (Cout, D), D), 'b2': jnp.zeros((Cout,), jnp.float32), 'alpha': jnp.ones((1,), jnp.float32), 'beta': jnp.zeros((1,), jnp.float32)}
    _L0_conv_all = _L0_conv_setup()
    _L0_conv_in = {k: v for k, v in _L0_conv_all.items() if k in ('W1', 'b1', 'Wv', 'bv', 'W2', 'b2', 'alpha', 'beta', )}
    del _L0_conv_all

    def _L1_conv_setup():
        import jax, jax.numpy as jnp
        import numpy as np
        WIN = 7
        HEADS = 6
        DIM = 192
        key = jax.random.key(seed)
        k0, k1, k2, k3 = jax.random.split(key, 4)
        B, C, H, W = (16, DIM, 56, 56)
        x = jax.random.normal(k0, (B, C, H, W), jnp.float32)
        qkv_w = jax.random.normal(k1, (3 * C, C), jnp.float32) * 0.02
        qkv_b = jnp.zeros((3 * C,), jnp.float32)
        proj_w = jax.random.normal(k2, (C, C), jnp.float32) * 0.02
        proj_b = jnp.zeros((C,), jnp.float32)
        bias_table = jax.random.normal(k3, (WIN * WIN, HEADS), jnp.float32) * 0.02
        return {'x': x, 'qkv_w': qkv_w, 'qkv_b': qkv_b, 'proj_w': proj_w, 'proj_b': proj_b, 'bias_table': bias_table}
    _L1_conv_all = _L1_conv_setup()
    _L1_conv_in = {k: v for k, v in _L1_conv_all.items() if k in ('qkv_w', 'qkv_b', 'proj_w', 'proj_b', 'bias_table', )}
    del _L1_conv_all

    return {
        "x": x,
        "L0_conv_W1": _L0_conv_in["W1"],
        "L0_conv_b1": _L0_conv_in["b1"],
        "L0_conv_Wv": _L0_conv_in["Wv"],
        "L0_conv_bv": _L0_conv_in["bv"],
        "L0_conv_W2": _L0_conv_in["W2"],
        "L0_conv_b2": _L0_conv_in["b2"],
        "L0_conv_alpha": _L0_conv_in["alpha"],
        "L0_conv_beta": _L0_conv_in["beta"],
        "L1_conv_qkv_w": _L1_conv_in["qkv_w"],
        "L1_conv_qkv_b": _L1_conv_in["qkv_b"],
        "L1_conv_proj_w": _L1_conv_in["proj_w"],
        "L1_conv_proj_b": _L1_conv_in["proj_b"],
        "L1_conv_bias_table": _L1_conv_in["bias_table"],
    }

def reference(x, L0_conv_W1, L0_conv_b1, L0_conv_Wv, L0_conv_bv, L0_conv_W2, L0_conv_b2, L0_conv_alpha, L0_conv_beta, L1_conv_qkv_w, L1_conv_qkv_b, L1_conv_proj_w, L1_conv_proj_b, L1_conv_bias_table):
    import jax
    import jax.numpy as jnp
    def _L0_conv_ref(x, W1, b1, Wv, bv, W2, b2, alpha, beta):
        import jax, jax.numpy as jnp
        import numpy as np
        HEADS, HEAD_DIM = (8, 32)
        FOLD_H, FOLD_W = (2, 2)
        PH, PW = (2, 2)
        EPS = 1e-12

        def conv1x1(x, W, b):
            return jnp.einsum('bchw,oc->bohw', x, W) + b[None, :, None, None]
        B, _, H, Wd = x.shape
        val = conv1x1(x, Wv, bv)
        xq = conv1x1(x, W1, b1)

        def split_fold(t):
            t = t.reshape(B * HEADS, HEAD_DIM, H, Wd)
            h, w = (H // FOLD_H, Wd // FOLD_W)
            t = t.reshape(B * HEADS, HEAD_DIM, FOLD_H, h, FOLD_W, w)
            t = t.transpose(0, 2, 4, 1, 3, 5).reshape(B * HEADS * FOLD_H * FOLD_W, HEAD_DIM, h, w)
            return t
        xq = split_fold(xq)
        val = split_fold(val)
        b, c, h, w = xq.shape
        N = h * w

        def adaptive_pool(t):
            return t.reshape(b, c, PH, h // PH, PW, w // PW).mean(axis=(3, 5))
        centers = adaptive_pool(xq).reshape(b, c, PH * PW).transpose(0, 2, 1)
        center_values = adaptive_pool(val).reshape(b, c, PH * PW).transpose(0, 2, 1)
        xf = xq.reshape(b, c, N).transpose(0, 2, 1)
        vf = val.reshape(b, c, N).transpose(0, 2, 1)
        cn = centers / jnp.clip(jnp.linalg.norm(centers, axis=-1, keepdims=True), EPS)
        xn = xf / jnp.clip(jnp.linalg.norm(xf, axis=-1, keepdims=True), EPS)
        sim = jax.nn.sigmoid(beta + alpha * jnp.einsum('bmc,bnc->bmn', cn, xn))
        idx = jnp.argmax(sim, axis=1)
        mask = jax.nn.one_hot(idx, PH * PW, axis=1, dtype=sim.dtype)
        sim = sim * mask
        agg = jnp.einsum('bmn,bnc->bmc', sim, vf) + center_values
        agg = agg / (mask.sum(axis=-1, keepdims=True) + 1.0)
        out = jnp.einsum('bmn,bmc->bnc', sim, agg)
        out = out.transpose(0, 2, 1).reshape(b, c, h, w)
        out = out.reshape(B * HEADS, FOLD_H, FOLD_W, c, h, w)
        out = out.transpose(0, 3, 1, 4, 2, 5).reshape(B * HEADS, c, H, Wd)
        out = out.reshape(B, HEADS * c, H, Wd)
        out = conv1x1(out, W2, b2)
        return out

    def _L1_conv_ref(x, qkv_w, qkv_b, proj_w, proj_b, bias_table):
        import jax, jax.numpy as jnp
        import numpy as np
        WIN = 7
        HEADS = 6
        DIM = 192
        B, C, H, W = x.shape
        heads, win = (HEADS, WIN)
        dh = C // heads
        p = win // 2
        scale = dh ** (-0.5)
        qkv = jnp.einsum('bcyx,oc->boyx', x, qkv_w) + qkv_b[None, :, None, None]
        q, k, v = (qkv[:, :C], qkv[:, C:2 * C], qkv[:, 2 * C:])
        q = (q * scale).reshape(B, heads, dh, H, W)
        kp = jnp.pad(k, ((0, 0), (0, 0), (p, p), (p, p))).reshape(B, heads, dh, H + win - 1, W + win - 1)
        vp = jnp.pad(v, ((0, 0), (0, 0), (p, p), (p, p))).reshape(B, heads, dh, H + win - 1, W + win - 1)
        attn = jnp.stack([jnp.einsum('bhdyx,bhdyx->bhyx', q, kp[:, :, :, i // win:i // win + H, i % win:i % win + W]) for i in range(win * win)], axis=2)
        attn = attn + bias_table.T[None, :, :, None, None]
        attn = jax.nn.softmax(attn, axis=2)
        out = jnp.zeros((B, heads, dh, H, W), x.dtype)
        for i in range(win * win):
            dy, dx = (i // win, i % win)
            out = out + attn[:, :, i][:, :, None] * vp[:, :, :, dy:dy + H, dx:dx + W]
        out = out.reshape(B, C, H, W)
        out = jnp.einsum('bcyx,oc->boyx', out, proj_w) + proj_b[None, :, None, None]
        return out

    def _gn(v, G=32, eps=1e-5):
        B_, C_, H_, W_ = v.shape
        g = v.reshape(B_, G, C_ // G, H_, W_)
        m = jnp.mean(g, axis=(2, 3, 4), keepdims=True)
        s = jnp.var(g, axis=(2, 3, 4), keepdims=True)
        return ((g - m) / jnp.sqrt(s + eps)).reshape(v.shape)

    def _ln_c(v, eps=1e-6):
        m = jnp.mean(v, axis=1, keepdims=True)
        s = jnp.var(v, axis=1, keepdims=True)
        return (v - m) / jnp.sqrt(s + eps)

    def _ln_t(v, eps=1e-5):
        m = jnp.mean(v, axis=-1, keepdims=True)
        s = jnp.var(v, axis=-1, keepdims=True)
        return (v - m) / jnp.sqrt(s + eps)

    def _to_tokens(v):
        B_, C_, H_, W_ = v.shape
        return v.reshape(B_, C_, H_ * W_).transpose(0, 2, 1)
    def _from_tokens(t, like):
        B_, C_, H_, W_ = like.shape
        return t.transpose(0, 2, 1).reshape(B_, C_, H_, W_)

    x = x + _L0_conv_ref(_gn(x), L0_conv_W1, L0_conv_b1, L0_conv_Wv, L0_conv_bv, L0_conv_W2, L0_conv_b2, L0_conv_alpha, L0_conv_beta)
    x = x + _L1_conv_ref(_gn(x), L1_conv_qkv_w, L1_conv_qkv_b, L1_conv_proj_w, L1_conv_proj_b, L1_conv_bias_table)
    return x


_drawn_inputs = setup_inputs


def setup_inputs(seed=0):
    import zlib

    import numpy as np

    out = dict(_drawn_inputs(seed))
    spreads = {'L0_conv_b1': (0.0, 1.298),
     'L0_conv_bv': (0.0, 0.267),
     'L0_conv_b2': (0.0, 0.1),
     'L1_conv_qkv_b': (0.0, 0.1),
     'L1_conv_proj_b': (0.0, 0.1)}
    factors = {'L1_conv_qkv_w': 4.592, 'L1_conv_bias_table': 33.127}
    for name, (base, spread) in spreads.items():
        noise = np.random.default_rng([zlib.crc32(name.encode()), seed]).standard_normal(out[name].shape)
        drawn = base * np.exp(spread * noise) if base else spread * noise
        out[name] = jnp.asarray(drawn.astype(out[name].dtype))
    for name, factor in factors.items():
        out[name] = (out[name] * factor).astype(out[name].dtype)
    return out
```

```python
import concourse.bass as bass
from concourse import mybir
from contextlib import ExitStack

F32 = mybir.dt.float32
ALU = mybir.AluOpType
ACT = mybir.ActivationFunctionType
AX = mybir.AxisListType

B, C, H, W = 32, 192, 56, 56
HC = C // 2
NPIX = H * W
GROUPS = 32
GC = C // GROUPS
EPS = 1e-5
HEADS0, D0 = 8, 256
FOLD = 28
POOL = 14
TR = 4
TT = FOLD // TR
TOK = TR * FOLD
HM = HEADS0 * 4
HEADS1, DH, WIN = 6, 32, 7
PAD = WIN // 2
WP = W + 2 * PAD
QB = 8
KB = QB + 2 * PAD
NK = KB * KB
NBAND = H // QB
STRIPS = NBAND + 1
HP = STRIPS * QB
KA = QB * KB
KBB = NK - KA
PAIRS = HEADS1 // 2
VW = 2 * DH + 1
BAND = QB * W
NEG = -1.0e30
UNITS = NBAND * PAIRS
ORDER = (0, 2, 1)
DUOS = (UNITS + 1) // 2
STEPS = NBAND * DUOS


def build(nc, x, w1t, w1n, wvt, w2t, b2, alpha, beta, qt, kt, qb, kb, vt, pt, pb, table, ident, gmat, hsum,
          hcol, hmask, fsel, cmask, tie, qscale, out, scratch):
    ctx = ExitStack()
    with ctx:
        def sb(name, shape):
            return ctx.enter_context(nc.sbuf_tensor(name, shape, F32))

        class Signal:

            def __init__(self, name, per, once=0):
                self.sem, self.per, self.once = ctx.enter_context(nc.semaphore(name)), per, once

            def at(self, img, k):
                return img * self.per + (self.once + k)

        xload = sb("xload", [HC, 2, NPIX])
        x1ext = sb("x1", [HC + 1, 2, NPIX])
        x1 = x1ext[0:HC, :, :]
        xtok = x1ext
        xpad = sb("xpad", [HC + 1, 2, HP * WP])
        kpad = sb("kpad", [128, 2, WP * WP])
        qbd = sb("qbd", [128, 2, 2, NBAND, 128])
        vring = sb("vring", [KA, 3, NBAND, PAIRS * VW])
        patch = sb("patch", [HC + 1, 2, NBAND, KA])
        msc = sb("msc", [128, 2, 2, NK])
        nmx = sb("nmx", [128, 2, 2])
        prob = sb("prob", [128, 3, 2, 2 * KA])
        probT = sb("probT", [128, 3, 512])
        orec = sb("orec", [128, 2, NBAND])
        otok = sb("otok", [128, NBAND, HC])
        ochan_s = sb("ochan", [128, 2 * BAND])
        ochan = ochan_s[0:HC, :].rearrange("p (e n) -> p e n", e=2)
        bmask = sb("bmask", [128, PAIRS, NK])
        w1t_s = sb("w1t_s", [HC + 1, 2, D0]); w1n_s = sb("w1n_s", [128, 2, C + 1])
        wvt_s = sb("wvt_s", [HC + 1, 2, D0]); w2t_s = sb("w2t_s", [128, 2, C])
        qt_s = sb("qt_s", [HC, 2, C]); kt_s = sb("kt_s", [HC, 2, C]); vt_s = sb("vt_s", [HC + 1, 2, C])
        pt_s = sb("pt_s", [HC, 2, C])
        cols = sb("cols", [128, 24])
        id_s = sb("id_s", [128, 128]); g_s = sb("g_s", [HC, HC]); hsum_s = sb("hsum_s", [128, 128])
        hcol_s = sb("hcol_s", [128, 2, HEADS0]); hmask_s = sb("hmask_s", [128, 2, 128])
        fsel_s = sb("fsel_s", [16, 128]); cmask_s = sb("cmask_s", [128, 16]); tie_s = sb("tie_s", [TOK, 4])
        halfs = sb("halfs", [128, TT * 4 * HEADS0])
        nhalf = sb("nhalf", [128, 2])
        ones = sb("ones", [128, 1])
        psums = sb("psums", [HC, 2, 16]); ssum = sb("ssum", [HC, 2]); nmean = sb("nmean", [HC, 2])
        ssq = sb("ssq", [HC, 2]); veps = sb("veps", [HC, 2]); rstd = sb("rstd", [HC, 2])
        nmr = sb("nmr", [HC, 2]); r196 = sb("r196", [HC, 2])
        pooled = sb("pooled", [HC + 1, 2, 16])
        cent = sb("cent", [128, 32]); csq = sb("csq", [128, 32]); cn2 = sb("cn2", [128, 32])
        cnrm = sb("cnrm", [128, 32]); cn = sb("cn", [128, 2, 16]); cbd = sb("cbd", [128, 2, 64])
        qsim = sb("qsim", [HC + 1, 2, 4, HM])
        sq = qbd[:, 0, :, :, :].rearrange("p h n q -> p (h n q)").rearrange("p (b m n) -> p b m n", b=2, m=2)
        n2 = sb("n2", [TOK, TT * 4 * HEADS0]); rn = sb("rn", [TOK, TT * 4 * HEADS0])
        mx = sb("mx", [TOK, TT * 4 * HEADS0])
        won = sb("won", [TOK, TT, 4, HM])
        sim = ochan_s[0:TOK, :].rearrange("p (t f n) -> p t f n", t=TT, f=4)
        key = probT[0:TOK, :, :].rearrange("p a b -> p (a b)")[:, 0:2 * BAND].rearrange("p (t f n) -> p t f n", t=TT, f=4)
        pooledT = sb("pooledT", [16, C + 1])
        xT = msc[0:TOK, :, :, :].rearrange("p a b n -> p (a b n)")[:, 0:4 * (C + 1)].rearrange("p (a b n) -> p a b n", a=2, b=2)
        rcnt = sb("rcnt", [128, 1]); ys = sb("ys", [128, C + 1]); ysT = sb("ysT", [HC + 1, 2, 128])
        agg = sb("agg", [128, 2, 128]); gout = sb("gout", [128, C]); simT = sb("simT", [128, TT * TOK])
        NA, NBETA = cols[0:TOK, 0:1], cols[0:TOK, 1:2]
        B2 = [cols[0:HC, 2 + t:3 + t] for t in range(2)]
        PB = [cols[0:HC, 4 + t:5 + t] for t in range(2)]
        QBIAS, KBIAS = (lambda t: cols[:, 6 + t:7 + t]), (lambda t: cols[:, 8 + t:9 + t])
        SCALE = [cols[:, 10 + e:11 + e] for e in range(2)]
        SBIAS = [[cols[:, 12 + 2 * t + e:13 + 2 * t + e] for e in range(2)] for t in range(2)]

        bank = [ctx.enter_context(nc.psum_tensor(f"bank{i}", [128, 512], F32)) for i in range(8)]
        psS, psT, psO, psX = bank[0:2], bank[2:4], bank[4:6], bank[6:8]
        psMisc, psDot, psN2, psF, psXT, psY = bank[0], bank[1:3], bank[3], bank[4:6], bank[6:8], bank[2]

        def interior(t, p=HC):
            return xpad[0:p, t, :].rearrange("p (r c) -> p r c", c=WP)[:, PAD:PAD + H, PAD:PAD + W]

        def tokens(t, p, tt, f):
            n = TOK * (4 * tt + f)
            return xtok[0:p, t, n:n + TOK]

        KP = (HC + 1, HC)

        s_const = Signal("consts_loaded", 0)
        s_init = Signal("fills_done", 0)
        s_fill = Signal("mask_filled", 0)
        s_scat = Signal("bias_scattered", 0)
        s_mask = Signal("mask_loaded", 0)
        s_rows = Signal("bias_rows_filled", 0)
        s_neg = Signal("alpha_beta_negated", 0)
        s_sbias = Signal("query_bias_scaled", 0)
        s_x = Signal("image_loaded", 32)
        s_xfree = Signal("image_used", 1)
        s_pool = Signal("pool_sums_ready", 1)
        s_sum = Signal("channel_sums_ready", 2)
        s_mean = Signal("group_means_ready", 2)
        s_nmean = Signal("minus_means_ready", 2)
        s_sq = Signal("square_sums_ready", 4)
        s_var = Signal("group_variances_ready", 2)
        s_veps = Signal("variance_eps_ready", 2)
        s_rstd = Signal("rstd_ready", 2)
        s_nmr = Signal("shift_ready", 3)
        s_norm = Signal("normalised", 4)
        s_pooled = Signal("pooled_ready", 1)
        s_cpsum = Signal("centres_projected", 1)
        s_cent = Signal("centres_copied", 1)
        s_csq = Signal("centre_squares_ready", 1)
        s_cn2 = Signal("centre_norms2_summed", 1)
        s_cn2s = Signal("centre_norms2_copied", 1)
        s_crt = Signal("centre_norms_ready", 1)
        s_cchain = Signal("centre_steps", 3)
        s_cbd = Signal("centres_spread", 1)
        s_qps = Signal("centres_in_pixel_space", 1)
        s_qsim = Signal("centre_columns_ready", 1)
        s_feat = Signal("features_ready", 14)
        s_fsq = Signal("feature_squares_ready", 14)
        s_sims = Signal("dots_and_norms_ready", 7)
        s_n2 = Signal("token_norms2_copied", 1)
        s_nrt = Signal("token_norms_ready", 1)
        s_rn = Signal("token_norm_steps", 2)
        s_z = Signal("cosines_ready", 1)
        s_e = Signal("sigmoid_exp_ready", 1)
        s_chain = Signal("argmax_steps", 7)
        s_won = Signal("similarities_masked", 1)
        s_pT = Signal("pooled_transposed", 1)
        s_pTs = Signal("pooled_transposed_copied", 1)
        s_xT = Signal("tokens_transposed", 14)
        s_xTs = Signal("tokens_transposed_copied", 14)
        s_y = Signal("cluster_sums_ready", 1)
        s_rc = Signal("count_steps", 2)
        s_ys = Signal("cluster_sums_scaled", 1)
        s_yT = Signal("cluster_sums_transposed", 1)
        s_yTs = Signal("cluster_sums_transposed_copied", 1)
        s_agg = Signal("clusters_projected", 1)
        s_aggs = Signal("clusters_masked", 1)
        s_g = Signal("cluster_outputs_ready", 1)
        s_gs = Signal("cluster_outputs_copied", 1)
        s_sT = Signal("similarities_transposed", 2)
        s_sTs = Signal("similarities_transposed_copied", 2)
        s_out0 = Signal("layer0_outputs_ready", 16)
        s_x1 = Signal("layer0_added", 16)

        s_patch = Signal("key_patches_copied", STRIPS)
        s_begun = {e: Signal(f"step_begun_by_{e}", 0) for e in ("dve", "pool")}
        s_scores = Signal("scores_ready", STEPS)
        s_max = Signal("maxima_ready", STEPS)
        s_exp = Signal("probabilities_ready", STEPS)
        s_tr = Signal("probabilities_transposed", STEPS)
        s_trs = Signal("probabilities_transposed_copied", STEPS)
        s_av = Signal("attention_ready", NBAND * PAIRS)
        s_rec = Signal("denominators_inverted", NBAND * PAIRS)
        s_on = Signal("attention_normalised", NBAND * PAIRS)

        jobs = {}

        def plan(step, kind, *arg):
            jobs.setdefault(step, []).append((kind, *arg))

        for half in range(2):
            plan(-1, "q", 0, half)
        for b in range(2):
            for half in range(2):
                plan(-1, "k", b, half)
            for n in range(4):
                plan(-1, "v", b, n)
        for b in range(NBAND):
            s = DUOS * b
            for half in range(2):
                if b + 1 < NBAND:
                    plan(s + 1, "q", b + 1, half)
                if b + 2 < NBAND:
                    plan(s + 3, "k", b + 2, half)
                plan(s + 19, "proj", b, half)
            if b + 2 <= NBAND:
                for n, at in enumerate((5, 6, 7, 9)):
                    plan(s + at, "v", b + 2, n)
            plan(s + 16, "o", b, 0)
            plan(s + 17, "o", b, 1)
        BY = {"q": "act", "k": "dve", "v": "dve", "o": "act", "proj": "dve"}
        order = [(s, job) for s in sorted(jobs) for job in jobs[s]]
        number = {job: n for n, (_, job) in enumerate(order)}
        emptied = []
        for _, job in order:
            emptied.append((BY[job[0]], 1 + sum(BY[j[0]] == BY[job[0]] for _, j in order[:len(emptied)])))
        LAST = STEPS + 10
        s_job = Signal("side_job_computed", len(order))
        s_emp = {e: Signal(f"side_job_emptied_by_{e}", sum(b == e for b, _ in emptied)) for e in ("act", "dve")}
        s_st = Signal("bands_stored", 16 * NBAND, once=16)
        finished = {}
        for g in range(NBAND * PAIRS):
            last_unit = NBAND * (g % PAIRS) + NBAND - 1
            finished.setdefault(DUOS * (g // PAIRS) + last_unit // 2, []).append(g)

        def units(d):
            b, j = divmod(d, DUOS)
            return [(b, u % NBAND, ORDER[u // NBAND]) for u in range(2 * j, min(2 * j + 2, UNITS))]

        everywhere = lambda a: bass.AP(a.tensor, 0, [[0, TOK], [1, 1]])
        consts = ((w1t_s[0:HC + 1, 0, :], w1t[0:HC + 1]), (w1t_s[0:HC, 1, :], w1t[HC + 1:C + 1]),
                  (w1n_s[:, :, :], w1n), (w2t_s[:, :, :], w2t),
                  (wvt_s[0:HC + 1, 0, :], wvt[0:HC + 1]), (wvt_s[0:HC, 1, :], wvt[HC + 1:C + 1]),
                  (vt_s[0:HC + 1, 0, :], vt[0:HC + 1]), (vt_s[0:HC, 1, :], vt[HC + 1:C + 1]),
                  (qt_s[:, :, :], qt), (kt_s[:, :, :], kt), (pt_s[:, :, :], pt),
                  (cols[0:TOK, 16:17], everywhere(alpha)), (cols[0:TOK, 17:18], everywhere(beta)),
                  (cols[0:HC, 2:4], b2), (cols[0:HC, 4:6], pb), (cols[:, 6:7], qb[0:128]),
                  (cols[0:64, 7:8], qb[128:C]), (cols[:, 8:9], kb[0:128]), (cols[0:64, 9:10], kb[128:C]),
                  (cols[:, 10:12], qscale), (id_s[:, :], ident), (g_s[:, :], gmat), (hsum_s[:, :], hsum),
                  (hcol_s[:, :, :], hcol), (hmask_s[:, :, :], hmask), (fsel_s[:, :], fsel), (cmask_s[:, :], cmask))
        CONSTS = 16 * len(consts)
        block = ctx.enter_context(nc.Block())

        @block.sync
        def _(sp):
            for dst, src in consts:
                sp.dma_start(dst, src).then_inc(s_const.sem, 16)
            sp.dma_start(tie_s[:, :], tie).then_inc(s_st.sem, 16)
            with sp.Fori(0, B) as img:
                sp.wait_ge(s_xfree.sem, s_xfree.at(img, 1))
                for t in range(2):
                    sp.dma_start(xload[:, t, :], x[bass.ds(img, 1), t * HC:(t + 1) * HC, :].rearrange("o p n -> (o p) n"))\
                        .then_inc(s_x.sem, 16)
                for b in range(NBAND):
                    sp.wait_ge(s_emp["dve"].sem, s_emp["dve"].at(img, emptied[number[("proj", b, 1)]][1]))
                    sp.dma_start(out[bass.ds(img, 1), :, b * BAND:(b + 1) * BAND].rearrange("o (t p) n -> (o p) t n", p=HC),
                                 x1[:, :, b * BAND:(b + 1) * BAND]).then_inc(s_st.sem, 16)
            sp.wait_ge(s_st.sem, 16 + 16 * NBAND * B)

        @block.gpsimd
        def _(pool):
            nc.gpsimd.memset(xpad[:, :, :], 0.0).then_inc(s_init.sem, 1)
            nc.gpsimd.memset(kpad[:, :, :], 0.0).then_inc(s_init.sem, 1)
            nc.gpsimd.memset(prob[:, :, :, :], 0.0).then_inc(s_init.sem, 1)
            nc.gpsimd.memset(vring[:, :, :, :], 1.0).then_inc(s_init.sem, 1)
            nc.gpsimd.memset(halfs[:, :], 0.5).then_inc(s_init.sem, 1)
            nc.gpsimd.memset(nhalf[:, :], -0.5).then_inc(s_init.sem, 1)
            nc.gpsimd.memset(ones[:, :], 1.0).then_inc(s_init.sem, 1)
            nc.gpsimd.memset(bmask[:, :, :], NEG).then_inc(s_fill.sem, 1)
            pool.wait_ge(s_fill.sem, 1)
            pool.dma_start(scratch.rearrange("(p n) -> p n", n=PAIRS * NK), bmask[:, :, :].rearrange("p a n -> p (a n)"))\
                .then_inc(s_scat.sem, 16)
            pool.wait_ge(s_scat.sem, 16)
            row = PAIRS * NK
            for par in range(2):
                for pair in range(PAIRS):
                    for r in range(QB):
                        first = (par * 64 + r * QB) * row + pair * NK + r * KB
                        dst = bass.AP(scratch.tensor, first, [[row + 1, QB], [KB, WIN], [1, WIN]])
                        head = 2 * pair + par
                        src = bass.AP(table.tensor, head * WIN * WIN, [[0, QB], [WIN, WIN], [1, WIN]])
                        pool.dma_start(dst, src).then_inc(s_scat.sem, 16)
            pool.wait_ge(s_scat.sem, 16 * (1 + 2 * PAIRS * QB))
            pool.dma_start(bmask[:, :, :].rearrange("p a n -> p (a n)"), scratch.rearrange("(p n) -> p n", n=row))\
                .then_inc(s_mask.sem, 16)

            pool.wait_ge(s_rows.sem, 3)
            with pool.Fori(0, B) as img:
                def power(g):
                    pool.wait_ge(s_veps.sem, s_veps.at(img, g + 1))
                    nc.gpsimd.tensor_tensor(rstd[:, :], veps[:, :], nhalf[0:HC, :], ALU.pow).then_inc(s_rstd.sem, 1)

                power(0)
                pool.wait_ge(s_cn2s.sem, s_cn2s.at(img, 1))
                nc.gpsimd.tensor_tensor(cnrm[:, :], cn2[:, :], halfs[:, 0:32], ALU.pow).then_inc(s_crt.sem, 1)
                pool.wait_ge(s_n2.sem, s_n2.at(img, 1))
                nc.gpsimd.tensor_tensor(rn[:, :], n2[:, :], halfs[0:TOK, :], ALU.pow).then_inc(s_nrt.sem, 1)
                power(1)
                for b in range(STRIPS):
                    if b == 0:
                        pool.wait_ge(s_norm.sem, s_norm.at(img, 4))
                    if b:
                        pool.wait_ge(s_job.sem, s_job.at(img, number[("v", b - 1, 3)] + 1))
                    pool.sem_inc(s_begun["pool"].sem, 1)
                    for c in range(NBAND):
                        src = xpad[:, :, :].rearrange("p t (r c) -> p t r c", c=WP)[:, :, QB * b:QB * b + QB, QB * c:QB * c + KB]
                        last = nc.gpsimd.tensor_copy(patch[:, :, c, :].rearrange("p t (r c) -> p t r c", c=KB), src)
                    last.then_inc(s_patch.sem, 1)

        @block.scalar
        def _(act):
            act.wait_ge(s_const.sem, CONSTS)
            act.wait_ge(s_init.sem, 7)
            for t, p in ((0, 128), (1, 64)):
                for e in range(2):
                    nc.scalar.activation(SBIAS[t][e][0:p], QBIAS(t)[0:p], ACT.Identity, bias=0.0,
                                         scale=SCALE[e][0:p]).then_inc(s_sbias.sem, 1)
            act.wait_ge(s_sbias.sem, 4)
            act.wait_ge(s_neg.sem, 1)

            with act.Fori(0, B) as img:
                def squares(g, src):
                    act.wait_ge(s_nmean.sem, s_nmean.at(img, g + 1))
                    for t in range(2):
                        nc.scalar.activation(interior(t), src[:, t, :].rearrange("p (r c) -> p r c", c=W), ACT.Square,
                                             bias=nmean[:, t:t + 1], scale=1.0, accum_out=ssq[:, t:t + 1])\
                            .then_inc(s_sq.sem, 1)

                squares(0, xload)
                for b in range(NBAND):
                    for m in range(2):
                        act.wait_ge(s_feat.sem, s_feat.at(img, 2 * b + m + 1))
                        if b >= 2:
                            act.wait_ge(s_sims.sem, s_sims.at(img, b - 1))
                        nc.scalar.activation(sq[:, b % 2, m, :], psF[m][:, 0:BAND], ACT.Square).then_inc(s_fsq.sem, 1)
                act.wait_ge(s_z.sem, s_z.at(img, 1))
                nc.scalar.activation(sim[:, :, :, :], key[:, :, :, :], ACT.Exp, bias=NBETA, scale=NA)\
                    .then_inc(s_e.sem, 1)
                for n in range(14):
                    act.wait_ge(s_xT.sem, s_xT.at(img, n + 1))
                    nc.scalar.activation(xT[:, n % 2, :, :], psXT[n % 2][0:TOK, 0:2 * (C + 1)].rearrange("p (n c) -> p n c", n=2),
                                         ACT.Copy).then_inc(s_xTs.sem, 1)
                for n in range(2):
                    act.wait_ge(s_sT.sem, s_sT.at(img, n + 1))
                    m = 4 * TOK if n == 0 else 3 * TOK
                    nc.scalar.activation(simT[:, 4 * TOK * n:4 * TOK * n + m], psXT[n][:, 0:m], ACT.Copy)\
                        .then_inc(s_sTs.sem, 1)

                squares(1, x1)

                def empty(n, job):
                    kind, b = job[0], job[1]
                    act.wait_ge(s_job.sem, s_job.at(img, n + 1))
                    ps = psX[n % 2]
                    if kind == "q":
                        half, p = job[2], (128, 64)[job[2]]
                        for e in range(2):
                            dst = qbd[0:p, b % 2, half, :, 64 * e:64 * e + 64].rearrange("p n (r c) -> p n r c", c=QB)
                            last = nc.scalar.activation(dst, ps[0:p, 0:BAND].rearrange("p (r n c) -> p n r c", n=NBAND, c=QB),
                                                        ACT.Identity, bias=SBIAS[half][e][0:p], scale=SCALE[e][0:p])
                    else:
                        c0, n4 = (0, 4) if job[2] == 0 else (4, 3)
                        for e in range(2):
                            src = ps[0:HC, 0:128 * n4].rearrange("p (n e r c) -> p e n r c", n=n4, e=2, c=QB)[:, e]
                            dst = ochan[:, e, :].rearrange("p (r n c) -> p n r c", n=NBAND, c=QB)[:, c0:c0 + n4]
                            last = nc.scalar.activation(dst, src, ACT.Copy)
                    last.then_inc(s_emp["act"].sem, 1)

                def empties(step):
                    for job in jobs.get(step, []):
                        if BY[job[0]] == "act":
                            empty(number[job], job)

                empties(-1)
                for step in range(LAST):
                    if step < STEPS:
                        act.wait_ge(s_max.sem, s_max.at(img, step + 1))
                        if step >= 3:
                            act.wait_ge(s_tr.sem, s_tr.at(img, step - 2))
                        for j in range(len(units(step))):
                            last = nc.scalar.activation(prob[:, step % 3, j, 0:NK], msc[:, step % 2, j, :], ACT.Exp,
                                                        bias=nmx[:, step % 2, j:j + 1], scale=-1.0)
                        last.then_inc(s_exp.sem, 1)
                    d = step - 2
                    if 0 <= d < STEPS:
                        n = 256 * len(units(d))
                        act.wait_ge(s_tr.sem, s_tr.at(img, d + 1))
                        nc.scalar.activation(probT[0:KA, d % 3, 0:n], psT[d % 2][0:KA, 0:n], ACT.Copy).then_inc(s_trs.sem, 1)
                    empties(step)

        @block.vector
        def _(dve):
            dve.wait_ge(s_const.sem, CONSTS)
            dve.wait_ge(s_init.sem, 7)
            nc.vector.memset(interior(0, HC + 1)[HC:HC + 1], 1.0).then_inc(s_rows.sem, 1)
            nc.vector.memset(xtok[HC:HC + 1, 0, :], 1.0).then_inc(s_rows.sem, 1)
            nc.vector.memset(pooled[HC:HC + 1, 0, :], 1.0).then_inc(s_rows.sem, 1)
            dve.wait_ge(s_mask.sem, 16)
            dve.wait_ge(s_st.sem, 16)
            nc.vector.tensor_scalar(cols[0:TOK, 0:2], cols[0:TOK, 16:18], -1.0, None, ALU.mult).then_inc(s_neg.sem, 1)
            nc.vector.memset(rcnt[0:1, :], 0.0).then_inc(s_xfree.sem, 1)
            with dve.Fori(0, B) as img:
                def stats(g, src):
                    t0 = psMisc[0:HC, 0:2]
                    if g == 0:
                        for t in range(2):
                            v = src[:, t, :].rearrange("p (a r b c) -> p a b r c", a=4, b=4, c=POOL)
                            last = nc.vector.tensor_reduce(psums[:, t, :].rearrange("p (a b) -> p a b", b=4), v, AX.XY, ALU.add)
                        last.then_inc(s_pool.sem, 1)
                        dve.wait_ge(s_pool.sem, s_pool.at(img, 1))
                        nc.vector.tensor_reduce(ssum[:, :], psums[:, :, :], AX.X, ALU.add).then_inc(s_sum.sem, 1)
                    else:
                        nc.vector.tensor_reduce(ssum[:, :], src[:, :, :], AX.X, ALU.add).then_inc(s_sum.sem, 1)
                    dve.wait_ge(s_mean.sem, s_mean.at(img, g + 1))
                    nc.vector.tensor_scalar(nmean[:, :], t0, -1.0, None, ALU.mult).then_inc(s_nmean.sem, 1)
                    dve.wait_ge(s_var.sem, s_var.at(img, g + 1))
                    nc.vector.tensor_scalar(veps[:, :], psMisc[0:HC, 2:4], EPS, None, ALU.add).then_inc(s_veps.sem, 1)
                    dve.wait_ge(s_rstd.sem, s_rstd.at(img, g + 1))
                    if g == 0:
                        nc.vector.tensor_scalar(r196[:, :], rstd[:, :], 1.0 / (POOL * POOL), None, ALU.mult)\
                            .then_inc(s_nmr.sem, 1)
                    nc.vector.tensor_tensor(nmr[:, :], nmean[:, :], rstd[:, :], ALU.mult).then_inc(s_nmr.sem, 1)
                    dve.wait_ge(s_nmr.sem, s_nmr.at(img, 2 + g))
                    if g == 0:
                        for t in range(2):
                            last = nc.vector.tensor_scalar(pooled[0:HC, t, :], psums[:, t, :], r196[:, t:t + 1],
                                                           nmr[:, t:t + 1], ALU.mult, ALU.add)
                        last.then_inc(s_pooled.sem, 1)
                    if g == 0:
                        dve.wait_ge(s_st.sem, s_st.at(img, 0))
                    for t in range(2):
                        pix = src[:, t, :].rearrange("p (r c) -> p r c", c=W)
                        if g == 0:
                            for f in range(4):
                                r, c = FOLD * (f // 2), FOLD * (f % 2)
                                last = nc.vector.tensor_scalar(
                                    xtok[0:HC, t, :].rearrange("p (a f r c) -> p f a r c", f=4, r=TR, c=FOLD)[:, f],
                                    pix[:, r:r + FOLD, c:c + FOLD].rearrange("p (a r) c -> p a r c", r=TR),
                                    rstd[:, t:t + 1], nmr[:, t:t + 1], ALU.mult, ALU.add)
                        else:
                            last = nc.vector.tensor_scalar(interior(t), pix, rstd[:, t:t + 1], nmr[:, t:t + 1],
                                                           ALU.mult, ALU.add)
                        last.then_inc(s_norm.sem, 1)

                dve.wait_ge(s_x.sem, s_x.at(img, 32))
                stats(0, xload)

                dve.wait_ge(s_cpsum.sem, s_cpsum.at(img, 1))
                nc.vector.tensor_copy(cent[:, :], psMisc[:, 8:40]).then_inc(s_cent.sem, 1)
                dve.wait_ge(s_cent.sem, s_cent.at(img, 1))
                nc.vector.tensor_tensor(csq[:, :], cent[:, :], cent[:, :], ALU.mult).then_inc(s_csq.sem, 1)
                dve.wait_ge(s_cn2.sem, s_cn2.at(img, 1))
                nc.vector.tensor_copy(cn2[:, :], psMisc[:, 40:72]).then_inc(s_cn2s.sem, 1)
                dve.wait_ge(s_crt.sem, s_crt.at(img, 1))
                nc.vector.tensor_scalar(cn2[:, :], cnrm[:, :], 1e-12, None, ALU.max).then_inc(s_cchain.sem, 1)
                dve.wait_ge(s_cchain.sem, s_cchain.at(img, 1))
                nc.vector.reciprocal(csq[:, :], cn2[:, :]).then_inc(s_cchain.sem, 1)
                dve.wait_ge(s_cchain.sem, s_cchain.at(img, 2))
                nc.vector.tensor_tensor(cn[:, :, :].rearrange("p m n -> p (m n)"), cent[:, :], csq[:, :], ALU.mult)\
                    .then_inc(s_cchain.sem, 1)
                dve.wait_ge(s_cchain.sem, s_cchain.at(img, 3))
                for m in range(2):
                    for f in range(4):
                        src = cn[:, m, :].rearrange("p (a u b v) -> p a b u v", a=2, u=2, b=2)[:, f // 2, f % 2]
                        src = src[:, None, :, :].broadcast_to([128, 4, 2, 2])
                        last = nc.vector.tensor_tensor(cbd[:, m, 16 * f:16 * f + 16].rearrange("p (h u v) -> p h u v", h=4, u=2),
                                                       src, cmask_s[:, :].rearrange("p (h u v) -> p h u v", h=4, u=2), ALU.mult)
                last.then_inc(s_cbd.sem, 1)
                dve.wait_ge(s_qps.sem, s_qps.at(img, 1))
                for t in range(2):
                    src = psMisc[0:KP[t], 128 + 128 * t:256 + 128 * t].rearrange("p (m f n) -> p m f n", m=2, f=4)
                    dst = qsim[0:KP[t], t, :, :].rearrange("p f (m n) -> p m f n", m=2)
                    last = nc.vector.tensor_copy(dst, src)
                last.then_inc(s_qsim.sem, 1)

                dve.wait_ge(s_sims.sem, s_sims.at(img, 7))
                nc.vector.tensor_copy(n2[:, :], psN2[0:TOK, 0:224]).then_inc(s_n2.sem, 1)
                dve.wait_ge(s_nrt.sem, s_nrt.at(img, 1))
                nc.vector.tensor_scalar(n2[:, :], rn[:, :], 1e-12, None, ALU.max).then_inc(s_rn.sem, 1)
                dve.wait_ge(s_rn.sem, s_rn.at(img, 1))
                nc.vector.reciprocal(rn[:, :], n2[:, :]).then_inc(s_rn.sem, 1)
                dve.wait_ge(s_rn.sem, s_rn.at(img, 2))
                flat = lambda a: a[:, :, :, :].rearrange("p t f (h m) -> p (t f h) m", m=4)
                for n, (lo, hi) in enumerate(((0, 128), (128, 224))):
                    last = nc.vector.tensor_tensor(flat(key)[:, lo:hi], psDot[n][0:TOK, 0:4 * (hi - lo)].rearrange("p (n m) -> p n m", m=4),
                                                   rn[:, lo:hi, None].broadcast_to([TOK, hi - lo, 4]), ALU.mult)
                last.then_inc(s_z.sem, 1)
                def step(k, ins):
                    ins.then_inc(s_chain.sem, 1)
                    dve.wait_ge(s_chain.sem, s_chain.at(img, k))

                top = mx[:, :, None].broadcast_to([TOK, 224, 4])
                dve.wait_ge(s_e.sem, s_e.at(img, 1))
                step(1, nc.vector.tensor_scalar(key[:, :, :, :], sim[:, :, :, :], 1.0, None, ALU.add))
                step(2, nc.vector.reciprocal(sim[:, :, :, :], key[:, :, :, :]))
                step(3, nc.vector.tensor_reduce(mx[:, :], flat(sim), AX.X, ALU.max))
                step(4, nc.vector.tensor_tensor(key[:, :, :, :].rearrange("p t f (h m) -> p (t f h) m", m=4), flat(sim), top, ALU.is_equal))
                step(5, nc.vector.tensor_tensor(flat(won), flat(key), tie_s[:, None, :].broadcast_to([TOK, 224, 4]), ALU.mult))
                step(6, nc.vector.tensor_reduce(mx[:, :], flat(won), AX.X, ALU.max))
                step(7, nc.vector.tensor_tensor(flat(key), flat(won), top, ALU.is_equal))
                nc.vector.tensor_tensor(won[:, :, :, :], sim[:, :, :, :], key[:, :, :, :], ALU.mult).then_inc(s_won.sem, 1)
                dve.wait_ge(s_pT.sem, s_pT.at(img, 1))
                nc.vector.tensor_copy(pooledT[:, :], psMisc[0:16, 0:C + 1]).then_inc(s_pTs.sem, 1)
                dve.wait_ge(s_y.sem, s_y.at(img, 1))
                nc.vector.tensor_scalar(rcnt[:, :], psN2[:, 256:257], 1.0, None, ALU.add).then_inc(s_rc.sem, 1)
                dve.wait_ge(s_rc.sem, s_rc.at(img, 1))
                nc.vector.reciprocal(rcnt[:, :], rcnt[:, :]).then_inc(s_rc.sem, 1)
                dve.wait_ge(s_rc.sem, s_rc.at(img, 2))
                nc.vector.tensor_scalar(ys[:, :], psY[:, 0:C + 1], rcnt[:, 0:1], None, ALU.mult).then_inc(s_ys.sem, 1)
                dve.wait_ge(s_yT.sem, s_yT.at(img, 1))
                nc.vector.tensor_copy(ysT[0:HC + 1, 0, :], psMisc[0:HC + 1, 0:128])
                nc.vector.tensor_copy(ysT[0:HC, 1, :], psMisc[0:HC, 128:256]).then_inc(s_yTs.sem, 1)
                dve.wait_ge(s_agg.sem, s_agg.at(img, 1))
                nc.vector.tensor_tensor(agg[:, :, :].rearrange("p m n -> p (m n)"), psMisc[:, 256:512],
                                        hmask_s[:, :, :].rearrange("p m n -> p (m n)"), ALU.mult).then_inc(s_aggs.sem, 1)
                dve.wait_ge(s_g.sem, s_g.at(img, 1))
                nc.vector.tensor_copy(gout[:, :], psMisc[:, 0:C]).then_inc(s_gs.sem, 1)
                n = 0
                for f in range(4):
                    for hf in range(2):
                        for t in range(2):
                            rows = 16 if hf == 0 else 12
                            r0, c0 = FOLD * (f // 2) + 16 * hf, FOLD * (f % 2)
                            pix = lambda a: a[:, t, :].rearrange("p (r c) -> p r c", c=W)[:, r0:r0 + rows, c0:c0 + FOLD]
                            dve.wait_ge(s_out0.sem, s_out0.at(img, n + 1))
                            nc.vector.scalar_tensor_tensor(pix(x1), psF[n % 2][0:HC, 0:rows * FOLD].rearrange("p (r c) -> p r c", c=FOLD),
                                                           B2[t], pix(xload), ALU.add, ALU.add).then_inc(s_x1.sem, 1)
                            n += 1
                dve.wait_ge(s_x1.sem, s_x1.at(img, 16))
                nc.vector.memset(rcnt[0:1, :], 0.0).then_inc(s_xfree.sem, 1)
                stats(1, x1)

                def empty(n, job):
                    kind, b = job[0], job[1]
                    dve.wait_ge(s_job.sem, s_job.at(img, n + 1))
                    ps = psX[n % 2]
                    if kind == "k":
                        half, p = job[2], (128, 64)[job[2]]
                        dst = kpad[0:p, half, :].rearrange("p (r c) -> p r c", c=WP)[:, PAD + QB * b:PAD + QB * b + QB, PAD:PAD + W]
                        last = nc.vector.tensor_scalar(dst, ps[0:p, 0:BAND].rearrange("p (r c) -> p r c", c=W),
                                                       KBIAS(half)[0:p], None, ALU.add)
                    elif kind == "v":
                        c0, m = 2 * job[2], min(2, NBAND - 2 * job[2])
                        dst = vring[:, b % 3, c0:c0 + m, :].rearrange("p n (a w) -> p (n a) w", w=VW)
                        src = ps[0:KA, 0:m * C].rearrange("p (a e c) -> p a e c", e=2, c=DH)
                        for e in range(2):
                            last = nc.vector.tensor_copy(dst[:, :, (DH + 1) * e:(DH + 1) * e + DH], src[:, :, e, :])
                    else:
                        t = job[2]
                        pix = x1[:, t, b * BAND:(b + 1) * BAND]
                        last = nc.vector.scalar_tensor_tensor(pix, ps[0:HC, 0:BAND], PB[t], pix, ALU.add, ALU.add)
                    last.then_inc(s_emp["dve"].sem, 1)

                def empties(step):
                    for job in jobs.get(step, []):
                        if BY[job[0]] == "dve":
                            empty(number[job], job)

                empties(-1)
                for step in range(LAST):
                    if step < STEPS:
                        dve.wait_ge(s_scores.sem, s_scores.at(img, step + 1))
                        if step >= 2:
                            dve.wait_ge(s_exp.sem, s_exp.at(img, step - 1))
                        dve.sem_inc(s_begun["dve"].sem, 1)
                        for j, (_, _, pair) in enumerate(units(step)):
                            last = nc.vector.tensor_tensor_reduce(
                                out=msc[:, step % 2, j, :], in0=psS[step % 2][:, j * NK:(j + 1) * NK], in1=bmask[:, pair, :],
                                scale=-1.0, scalar=3.0e38, op0=ALU.add, op1=ALU.min, accum_out=nmx[:, step % 2, j:j + 1])
                        last.then_inc(s_max.sem, 1)
                    for g in finished.get(step - 4, []):
                        ps = psO[g % 2]
                        dve.wait_ge(s_av.sem, s_av.at(img, g + 1))
                        v = ps[:, 0:NBAND * VW].rearrange("p (n w) -> p n w", w=VW)
                        nc.vector.reciprocal(orec[:, g % 2, :], v[:, :, DH]).then_inc(s_rec.sem, 1)
                        dve.wait_ge(s_rec.sem, s_rec.at(img, g + 1))
                        pair = ORDER[g % PAIRS]
                        for e in range(2):
                            q = slice(64 * e, 64 * e + 64)
                            last = nc.vector.tensor_tensor(
                                otok[q, :, DH * pair:DH * pair + DH], v[q, :, (DH + 1) * e:(DH + 1) * e + DH],
                                orec[q, g % 2, :, None].broadcast_to([64, NBAND, DH]), ALU.mult)
                        last.then_inc(s_on.sem, 1)
                    empties(step)

        @block.tensor
        def _(pe):
            mm = nc.tensor.matmul
            pe.wait_ge(s_const.sem, CONSTS)
            pe.wait_ge(s_init.sem, 7)
            pe.wait_ge(s_rows.sem, 3)
            with pe.Fori(0, B) as img:
                def stats(g):
                    pe.wait_ge(s_sum.sem, s_sum.at(img, g + 1))
                    mm(psMisc[0:HC, 0:2], g_s[:, :], ssum[:, :], start=True, stop=True).then_inc(s_mean.sem, 1)
                    pe.wait_ge(s_sq.sem, s_sq.at(img, 2 * g + 2))
                    pe.wait_ge(s_nmean.sem, s_nmean.at(img, g + 1))
                    mm(psMisc[0:HC, 2:4], g_s[:, :], ssq[:, :], start=True, stop=True).then_inc(s_var.sem, 1)

                stats(0)
                pe.wait_ge(s_veps.sem, s_veps.at(img, 1))
                pe.wait_ge(s_pooled.sem, s_pooled.at(img, 1))
                for m in range(2):
                    for t in range(2):
                        last = mm(psMisc[:, 8 + 16 * m:24 + 16 * m], w1t_s[0:KP[t], t, 128 * m:128 * m + 128],
                                  pooled[0:KP[t], t, :], start=(t == 0), stop=(t == 1))
                last.then_inc(s_cpsum.sem, 1)
                pe.wait_ge(s_csq.sem, s_csq.at(img, 1))
                mm(psMisc[:, 40:72], hsum_s[:, :], csq[:, :], start=True, stop=True).then_inc(s_cn2.sem, 1)
                pe.wait_ge(s_cbd.sem, s_cbd.at(img, 1))
                for t in range(2):
                    for m in range(2):
                        last = mm(psMisc[0:KP[t], 128 + 128 * t + 64 * m:192 + 128 * t + 64 * m],
                                  w1n_s[:, m, (HC + 1) * t:(HC + 1) * t + KP[t]], cbd[:, m, :], start=True, stop=True)
                last.then_inc(s_qps.sem, 1)
                pe.wait_ge(s_norm.sem, s_norm.at(img, 2))

                def features(b):
                    for m in range(2):
                        if b:
                            pe.wait_ge(s_fsq.sem, s_fsq.at(img, 2 * b - 1 + m))
                        for t in range(2):
                            last = mm(psF[m][:, 0:BAND], w1t_s[0:KP[t], t, 128 * m:128 * m + 128],
                                      xtok[0:KP[t], t, BAND * b:BAND * b + BAND], start=(t == 0), stop=(t == 1))
                        last.then_inc(s_feat.sem, 1)

                features(0)
                pe.wait_ge(s_qsim.sem, s_qsim.at(img, 1))
                for b in range(NBAND):
                    if b + 1 < NBAND:
                        features(b + 1)
                    pe.wait_ge(s_fsq.sem, s_fsq.at(img, 2 * b + 2))
                    for f in range(4):
                        n = 4 * b + f
                        for m in range(2):
                            mm(psN2[0:TOK, HEADS0 * n:HEADS0 * n + HEADS0], sq[:, b % 2, m, TOK * f:TOK * f + TOK],
                               hcol_s[:, m, :], start=(m == 0), stop=(m == 1))
                        for t in range(2):
                            last = mm(psDot[n // 16][0:TOK, HM * (n % 16):HM * (n % 16) + HM], tokens(t, KP[t], b, f),
                                      qsim[0:KP[t], t, f, :], start=(t == 0), stop=(t == 1))
                    last.then_inc(s_sims.sem, 1)
                mm_t = nc.tensor.transpose
                mm_t(psMisc[0:16, 0:HC + 1], pooled[0:HC + 1, 0, :], id_s[0:HC + 1, 0:HC + 1])
                mm_t(psMisc[0:16, HC + 1:C + 1], pooled[0:HC, 1, :], id_s[0:HC, 0:HC]).then_inc(s_pT.sem, 1)

                def by_token(n):
                    tt, f = divmod(2 * n, 4)
                    if n >= 2:
                        pe.wait_ge(s_xTs.sem, s_xTs.at(img, n - 1))
                    for j in range(2):
                        o = (C + 1) * j
                        mm_t(psXT[n % 2][0:TOK, o:o + HC + 1], tokens(0, HC + 1, tt, f + j), id_s[0:HC + 1, 0:HC + 1])
                        last = mm_t(psXT[n % 2][0:TOK, o + HC + 1:o + C + 1], tokens(1, HC, tt, f + j), id_s[0:HC, 0:HC])
                    last.then_inc(s_xT.sem, 1)

                by_token(0)
                by_token(1)
                pe.wait_ge(s_won.sem, s_won.at(img, 1))
                pe.wait_ge(s_pTs.sem, s_pTs.at(img, 1))
                mm(psY[:, 0:C + 1], fsel_s[:, :], pooledT[:, :], start=True, stop=False, skip_group_check=True)
                for n in range(14):
                    pe.wait_ge(s_xTs.sem, s_xTs.at(img, n + 1))
                    for j in range(2):
                        tt, f = divmod(2 * n + j, 4)
                        mm(psY[HM * f:HM * f + HM, 0:C + 1], won[:, tt, f, :], xT[:, n % 2, j, :], start=False,
                           stop=(n == 13), skip_group_check=True)
                    if n + 2 < 14:
                        by_token(n + 2)
                for f in range(4):
                    for tt in range(TT):
                        last = mm(psN2[HM * f:HM * f + HM, 256:257], key[:, tt, f, :], ones[0:TOK, :], start=(tt == 0),
                                  stop=(tt == TT - 1))
                last.then_inc(s_y.sem, 1)
                for n in range(2):
                    for tt in range(4 * n, min(4 * n + 4, TT)):
                        last = mm_t(psXT[n][:, TOK * (tt % 4):TOK * (tt % 4) + TOK],
                                    won[:, tt, :, :].rearrange("p f n -> p (f n)"), id_s[0:TOK, 0:TOK])
                    last.then_inc(s_sT.sem, 1)
                pe.wait_ge(s_ys.sem, s_ys.at(img, 1))
                mm_t(psMisc[0:HC + 1, 0:128], ys[:, 0:HC + 1], id_s[:, :])
                mm_t(psMisc[0:HC, 128:256], ys[:, HC + 1:C + 1], id_s[:, :]).then_inc(s_yT.sem, 1)
                pe.wait_ge(s_yTs.sem, s_yTs.at(img, 1))
                for m in range(2):
                    for t in range(2):
                        last = mm(psMisc[:, 256 + 128 * m:384 + 128 * m], wvt_s[0:KP[t], t, 128 * m:128 * m + 128],
                                  ysT[0:KP[t], t, :], start=(t == 0), stop=(t == 1))
                last.then_inc(s_agg.sem, 1)
                pe.wait_ge(s_aggs.sem, s_aggs.at(img, 1))
                for m in range(2):
                    last = mm(psMisc[:, 0:C], agg[:, m, :], w2t_s[:, m, :], start=(m == 0), stop=(m == 1))
                last.then_inc(s_g.sem, 1)
                pe.wait_ge(s_gs.sem, s_gs.at(img, 1))
                pe.wait_ge(s_sTs.sem, s_sTs.at(img, 2))
                n = 0
                for f in range(4):
                    for hf in range(2):
                        for t in range(2):
                            m = 4 * TOK if hf == 0 else 3 * TOK
                            if n >= 2:
                                pe.wait_ge(s_x1.sem, s_x1.at(img, n - 1))
                            q = slice(HM * f, HM * f + HM)
                            mm(psF[n % 2][0:HC, 0:m], gout[q, HC * t:HC * t + HC], simT[q, 4 * TOK * hf:4 * TOK * hf + m],
                               start=True, stop=True).then_inc(s_out0.sem, 1)
                            n += 1
                stats(1)
                pe.wait_ge(s_norm.sem, s_norm.at(img, 4))

                def compute(n, job):
                    kind, b = job[0], job[1]
                    if n >= 2:
                        e, k = emptied[n - 2]
                        pe.wait_ge(s_emp[e].sem, s_emp[e].at(img, k))
                    ps = psX[n % 2]
                    if kind in "qk":
                        half, p = job[2], (128, 64)[job[2]]
                        w = qt_s if kind == "q" else kt_s
                        for t in range(2):
                            last = mm(ps[0:p, 0:BAND], w[:, t, 128 * half:128 * half + p],
                                      interior(t)[:, QB * b:QB * b + QB, :], start=(t == 0), stop=(t == 1))
                    elif kind == "v":
                        pe.wait_ge(s_patch.sem, s_patch.at(img, b + 1))
                        for j in range(min(2, NBAND - 2 * job[2])):
                            c = 2 * job[2] + j
                            for t in range(2):
                                last = mm(ps[0:KA, C * j:C * j + C], patch[0:KP[t], t, c, :], vt_s[0:KP[t], t, :], start=(t == 0), stop=(t == 1))
                    elif kind == "o":
                        c0, n4 = (0, 4) if job[2] == 0 else (4, 3)
                        pe.wait_ge(s_on.sem, s_on.at(img, PAIRS * (b + 1)))
                        for j in range(n4):
                            last = mm_t(ps[0:HC, 128 * j:128 * j + 128], otok[:, c0 + j, :], id_s[:, :])
                    else:
                        t = job[2]
                        e, k = emptied[number[("o", b, 1)]]
                        pe.wait_ge(s_emp[e].sem, s_emp[e].at(img, k))
                        for e in range(2):
                            last = mm(ps[0:HC, 0:BAND], pt_s[:, e, HC * t:HC * t + HC], ochan[:, e, :], start=(e == 0), stop=(e == 1))
                    last.then_inc(s_job.sem, 1)

                for job in jobs[-1]:
                    compute(number[job], job)
                for step in range(LAST):
                    if step < STEPS:
                        if step % DUOS == 0:
                            for e in ("act", "dve"):
                                done = [emptied[number[j]][1] for s in jobs if s < step for j in jobs[s] if BY[j[0]] == e]
                                pe.wait_ge(s_emp[e].sem, s_emp[e].at(img, max(done)))
                        if step >= 2:
                            pe.wait_ge(s_max.sem, s_max.at(img, step - 1))
                        for j, (b, c, pair) in enumerate(units(step)):
                            half, p0 = pair // 2, 64 * (pair % 2)
                            keys = kpad[p0:p0 + 64, half, :].rearrange("p (r c) -> p r c", c=WP)[:, QB * b:QB * b + KB, QB * c:QB * c + KB]
                            last = mm(psS[step % 2][:, j * NK:(j + 1) * NK], qbd[p0:p0 + 64, b % 2, half, c, :], keys,
                                      start=True, stop=True)
                        last.then_inc(s_scores.sem, 1)
                    for job in jobs.get(step, []):
                        compute(number[job], job)
                    d = step - 2
                    if 0 <= d < STEPS:
                        pe.wait_ge(s_exp.sem, s_exp.at(img, d + 1))
                        if d >= 2:
                            pe.wait_ge(s_trs.sem, s_trs.at(img, d - 1))
                        for j in range(len(units(d))):
                            for k in range(2):
                                last = mm_t(psT[d % 2][0:KA, 256 * j + 128 * k:256 * j + 128 * k + 128],
                                            prob[:, d % 3, j, KA * k:KA * k + KA], id_s[:, :])
                        last.then_inc(s_tr.sem, 1)
                    d = step - 3
                    if 0 <= d < STEPS:
                        pe.wait_ge(s_trs.sem, s_trs.at(img, d + 1))
                        for j, (b, c, pair) in enumerate(units(d)):
                            g = PAIRS * b + ORDER.index(pair)
                            if c == 0 and g >= 2:
                                pe.wait_ge(s_on.sem, s_on.at(img, g - 1))
                            for k, p in enumerate((KA, KBB)):
                                last = mm(psO[g % 2][:, VW * c:VW * c + VW],
                                          probT[0:p, d % 3, 256 * j + 128 * k:256 * j + 128 * k + 128],
                                          vring[0:p, (b + k) % 3, c, VW * pair:VW * pair + VW], start=(k == 0), stop=(k == 1))
                            if c == NBAND - 1:
                                last.then_inc(s_av.sem, 1)


def kernel(x, L0_conv_W1, L0_conv_b1, L0_conv_Wv, L0_conv_bv, L0_conv_W2, L0_conv_b2, L0_conv_alpha, L0_conv_beta,
           L1_conv_qkv_w, L1_conv_qkv_b, L1_conv_proj_w, L1_conv_proj_b, L1_conv_bias_table):
    import numpy as np
    import concourse.bacc as bacc
    from concourse.bass_utils import run_bass_kernel_spmd

    def halves(wt):
        return np.ascontiguousarray(np.asarray(wt).reshape(2, HC, -1).transpose(1, 0, 2))

    def with_bias(wt, b):
        wt, b = np.asarray(wt), np.asarray(b)
        return np.concatenate([wt[:HC], b[None, :], wt[HC:]], 0)

    W1, W2, Wv, qkv, proj = (np.asarray(a) for a in (L0_conv_W1, L0_conv_W2, L0_conv_Wv, L1_conv_qkv_w, L1_conv_proj_w))
    qkv_b = np.asarray(L1_conv_qkv_b)
    w1n = np.concatenate([W1[:, :HC], np.asarray(L0_conv_b1)[:, None], W1[:, HC:]], 1)
    projT = proj.T.reshape(PAIRS, 2, DH, C).transpose(0, 2, 1, 3).reshape(HC, 2, C)
    f = np.float32
    p = np.arange(128)
    chan = np.arange(HC)
    gmat = ((chan[:, None] // GC) == (chan[None, :] // GC)).astype(f) / f(GC * NPIX)
    hsum = ((p[:, None] // 32) == (p[None, :] // 32)).astype(f)
    hcol = np.stack([((4 * m + p[:, None] // 32) == np.arange(HEADS0)[None, :]).astype(f) for m in range(2)], 1)
    fhm = np.arange(128)
    hmask = np.stack([((4 * m + p[:, None] // 32) == ((fhm % 32) // 4)[None, :]).astype(f) for m in range(2)], 1)
    rc = np.arange(16)
    R, Cc = rc // 4, rc % 4
    fold, cen = 2 * (R // 2) + Cc // 2, 2 * (R % 2) + Cc % 2
    fsel = ((fold[:, None] == (fhm // 32)[None, :]) & (cen[:, None] == (fhm % 4)[None, :])).astype(f)
    cmask = ((p[:, None] // 32) == (np.arange(16) // 4)[None, :]).astype(f)
    tie = np.broadcast_to(np.array([4, 3, 2, 1], f), (TOK, 4))
    qscale = np.stack([((p // 32) % 2 == e).astype(f) * f(DH ** -0.5) for e in range(2)], 1)
    arrays = {
        "x": np.asarray(x).reshape(B, C, NPIX),
        "w1t": with_bias(W1.T, L0_conv_b1), "w1n": w1n.reshape(2, 128, C + 1).transpose(1, 0, 2),
        "wvt": with_bias(Wv.T, L0_conv_bv), "w2t": W2.T.reshape(2, 128, C).transpose(1, 0, 2),
        "b2": np.asarray(L0_conv_b2).reshape(2, HC).T,
        "alpha": np.asarray(L0_conv_alpha).reshape(1, 1), "beta": np.asarray(L0_conv_beta).reshape(1, 1),
        "qt": halves(qkv[:C].T), "kt": halves(qkv[C:2 * C].T), "qb": qkv_b[:C, None], "kb": qkv_b[C:2 * C, None],
        "vt": with_bias(qkv[2 * C:].T, qkv_b[2 * C:]), "pt": projT,
        "pb": np.asarray(L1_conv_proj_b).reshape(2, HC).T, "table": np.asarray(L1_conv_bias_table).T,
        "ident": np.eye(128, dtype=f), "gmat": gmat, "hsum": hsum, "hcol": hcol, "hmask": hmask, "fsel": fsel,
        "cmask": cmask, "tie": tie, "qscale": qscale,
    }
    nc = bacc.Bacc("TRN2", target_bir_lowering=False, num_devices=1)
    ins = {}
    arrays = {f"in_{k}": np.ascontiguousarray(v) for k, v in arrays.items()}
    for k, v in arrays.items():
        ins[k[3:]] = nc.dram_tensor(k, v.shape, mybir.dt.from_np(v.dtype), kind="ExternalInput").ap()
    out = nc.dram_tensor("out_0", (B, C, NPIX), F32, kind="ExternalOutput").ap()
    scratch = nc.dram_tensor("mask_scratch", (128 * PAIRS * NK,), F32, kind="Internal").ap()
    build(nc, out=out, scratch=scratch, **ins)
    r = run_bass_kernel_spmd(nc, [arrays], core_ids=[0])
    return r.results[0]["out_0"].reshape(B, C, H, W)
```

```python
import concourse.bass as bass
from concourse import mybir
from contextlib import ExitStack

F32 = mybir.dt.float32
ALU = mybir.AluOpType
ACT = mybir.ActivationFunctionType
AX = mybir.AxisListType

B, C, H, W = 32, 192, 56, 56
HC = C // 2
NPIX = H * W
GROUPS = 32
GC = C // GROUPS
EPS = 1e-5
HEADS0, D0 = 8, 256
FOLD = 28
POOL = 14
TR = 4
TT = FOLD // TR
TOK = TR * FOLD
HM = HEADS0 * 4
HEADS1, DH, WIN = 6, 32, 7
PAD = WIN // 2
WP = W + 2 * PAD
QB = 8
KB = QB + 2 * PAD
NK = KB * KB
NBAND = H // QB
STRIPS = NBAND + 1
HP = STRIPS * QB
KA = QB * KB
KBB = NK - KA
PAIRS = HEADS1 // 2
VW = 2 * DH + 1
BAND = QB * W
NEG = -1.0e30
UNITS = NBAND * PAIRS
ORDER = (0, 2, 1)
DUOS = (UNITS + 1) // 2
STEPS = NBAND * DUOS

PERIOD = 6
CHUNK0 = 15
END0 = CHUNK0 + PERIOD * (TT - 1) + 9
OUT0 = END0 + 4
STAT1 = OUT0 + 8
HEAD1 = STAT1 + 7
SLOTS = HEAD1 + 8
PIECES = 4
PIECE = NPIX // PIECES


def schedule():
    slots = [[] for _ in range(SLOTS)]
    for b in range(NBAND):
        s = DUOS * b
        if b + 2 < NBAND:
            slots[s + 1] += [(0, "qk", b + 2, 0), (0, "qk", b + 2, 1)]
            slots[s + 2] += [(0, "qk", b + 2, 2)]
        if b + 2 < STRIPS:
            for n, at in enumerate((4, 6, 7, 9)):
                slots[s + at].append((0, "v", b + 2, n))
        slots[s + 16].append((0, "o", b, 0))
        slots[s + 17].append((0, "o", b, 1))
        for half in range(2):
            slots[s + 19].append((0, "proj", b, half))
    slots[7].append((1, "mean", 0))
    slots[10].append((1, "var", 0))
    slots[13].append((1, "centres"))
    slots[14].append((1, "norms"))
    slots[17].append((1, "pixels"))
    for n in reversed(range(TT)):
        c = CHUNK0 + PERIOD * n
        slots[c + 1] += [(1, "feat", n, 0), (1, "feat", n, 1)]
        slots[c + 2] += [(1, "tok", n, 0), (1, "tok", n, 1)]
        slots[c + 3].append((1, "dots", n))
        slots[c + 8].insert(0, (1, "sums", n))
    slots[END0 + 1].append((1, "sumsT"))
    slots[END0 + 2].append((1, "agg"))
    slots[END0 + 3].append((1, "gout"))
    for n in range(16):
        slots[OUT0 + n // 2].append((1, "out0", n))
    slots[STAT1 + 1].append((1, "mean", 1))
    slots[STAT1 + 4].append((1, "var", 1))
    for b in range(2):
        for k in range(3):
            slots[HEAD1 + b].append((1, "qk", b, k))
        for n in range(4):
            slots[HEAD1 + 2 + 2 * b + n // 2].append((1, "v", b, n))
    return slots


JOBS = schedule()
BY = {"qk": ("act", "dve", "act"), "v": "dve", "o": "act", "proj": "dve", "mean": "dve", "var": "dve",
      "centres": "dve", "norms": "dve", "pixels": "dve", "feat": "act", "tok": "act", "dots": "dve",
      "sums": "dve", "sumsT": "dve", "agg": "dve", "gout": "dve", "out0": "dve"}


def emptier(job):
    by = BY[job[1]]
    return by if isinstance(by, str) else by[job[3]]


ORDERED = [job for jobs in JOBS for job in jobs]
BANK = {job: n % 2 for n, job in enumerate(ORDERED)}
NTH = {job: 1 + sum(j[0] == job[0] for j in ORDERED[:n]) for n, job in enumerate(ORDERED)}
NTH_BY = {job: 1 + sum(j[0] == job[0] and emptier(j) == emptier(job) for j in ORDERED[:n])
          for n, job in enumerate(ORDERED)}


def before(job, turns):
    ran = [j for j in ORDERED if j[0] in turns]
    had = [j for j in ran[:ran.index(job)] if BANK[j] == BANK[job]]
    return had[-1] if had else None


def build(nc, x, w1t, w1n, wvt, w2t, b2, alpha, beta, qk, qb, kb, vt, pt, pb, table, ident, gmat, hsum,
          hcol, hmask, fsel, cmask, tie, qscale, out, scratch):
    ctx = ExitStack()
    with ctx:
        def sb(name, shape, dt=F32):
            return ctx.enter_context(nc.sbuf_tensor(name, shape, dt))

        class Signal:

            def __init__(self, name, per, once=0):
                self.sem, self.per, self.once = ctx.enter_context(nc.semaphore(name)), per, once

            def at(self, img, k):
                return img * self.per + (self.once + k)

        KP = (HC + 1, HC)

        xbuf = [sb(f"xbuf{n}", [HC + 1, 2, NPIX]) for n in range(2)]
        xband = sb("xband", [HC, 2, 2, BAND])
        patch = sb("patch", [HC + 1, 2, 2, NBAND, KA])
        kpad = sb("kpad", [128, 2, WP * WP])
        qbd = sb("qbd", [128, 3, 2, NBAND, 128])
        vring = sb("vring", [KA, 3, NBAND, PAIRS * VW])
        msc = sb("msc", [128, 2, 2, NK])
        nmx = sb("nmx", [128, 2, 2])
        prob = sb("prob", [128, 3, 2, 2 * KA])
        probT = sb("probT", [KA, 2, 512])
        orec = sb("orec", [128, 2, NBAND])
        otok = sb("otok", [128, NBAND, HC])
        ochan = sb("ochan", [HC, 2, BAND])
        bmask = sb("bmask", [128, PAIRS, NK])
        w1t_s = sb("w1t_s", [HC + 1, 2, D0]); w1n_s = sb("w1n_s", [128, 2, C + 1])
        wvt_s = sb("wvt_s", [HC + 1, 2, D0]); w2t_s = sb("w2t_s", [128, 2, C])
        qk_s = sb("qk_s", [HC, 2, 2 * C]); vt_s = sb("vt_s", [HC + 1, 2, C]); pt_s = sb("pt_s", [HC, 2, C])
        cols = sb("cols", [128, 24])
        id_s = sb("id_s", [128, 128]); g_s = sb("g_s", [HC, HC]); hsum_s = sb("hsum_s", [128, 128])
        hcol_s = sb("hcol_s", [128, 2, HEADS0]); hmask_s = sb("hmask_s", [128, 2, 128])
        fsel_s = sb("fsel_s", [16, 128]); cmask_s = sb("cmask_s", [128, 16]); tie_s = sb("tie_s", [TOK, 4])
        halfs = sb("halfs", [128, 32])
        nhalf = sb("nhalf", [128, 2])
        ones = sb("ones", [128, 1])
        psums = sb("psums", [HC, 2, 16]); ssum = sb("ssum", [HC, 2]); nmean = sb("nmean", [HC, 2])
        ssq = sb("ssq", [HC, 2 * PIECES]); veps = sb("veps", [HC, 2, 2]); osum = sb("osum", [HC, 2, 8])
        rstd = sb("rstd", [HC + 1, 2, 2]); nmr = sb("nmr", [HC + 1, 2, 2]); r196 = sb("r196", [HC, 2])
        junk = sb("junk", [HC, PIECE], mybir.dt.bfloat16)
        pooled = sb("pooled", [HC + 1, 2, 16]); pooledT = sb("pooledT", [16, C + 1])
        cent = sb("cent", [128, 32]); csq = sb("csq", [128, 32]); cn2 = sb("cn2", [128, 32])
        cnrm = sb("cnrm", [128, 32]); cn = sb("cn", [128, 2, 16]); cbd = sb("cbd", [128, 2, 64])
        qsim = sb("qsim", [HC + 1, 2, 4, HM])
        xtok = sb("xtok", [HC + 1, 2, 2, BAND])
        sq = sb("sq", [128, 2, BAND])
        nd = sb("nd", [TOK, 32 + 128])
        rn = sb("rn", [TOK, 32]); rm = sb("rm", [TOK, 32]); zz = sb("zz", [TOK, 128]); ee = sb("ee", [TOK, 128])
        mx = sb("mx", [TOK, 32]); sim = sb("sim", [TOK, 128]); key = sb("key", [TOK, 128]); won = sb("won", [TOK, 128])
        xT = sb("xT", [TOK, 4, C + 1])
        yacc = sb("yacc", [128, C + 2])
        rcnt = sb("rcnt", [128, 2]); ys = sb("ys", [128, C + 1]); ysT = sb("ysT", [HC + 1, 2, 128])
        agg = sb("agg", [128, 2, 128]); gout = sb("gout", [128, C]); simT = sb("simT", [128, TT * TOK])
        NA, NBETA = cols[0:TOK, 0:1], cols[0:TOK, 1:2]
        B2 = [cols[0:HC, 2 + t:3 + t] for t in range(2)]
        PB = [cols[0:HC, 4 + t:5 + t] for t in range(2)]
        SCALE = [cols[:, 10 + e:11 + e] for e in range(2)]
        QBIAS, KBIAS = (lambda t: cols[:, 6 + t:7 + t]), (lambda t: cols[:, 8 + t:9 + t])
        SBIAS = [[cols[:, 12 + 2 * t + e:13 + 2 * t + e] for e in range(2)] for t in range(2)]

        bank = [ctx.enter_context(nc.psum_tensor(f"bank{i}", [128, 512], F32)) for i in range(8)]
        psS, psT, psO, psX = bank[0:2], bank[2:4], bank[4:6], bank[6:8]

        def rows(a, w=W):
            return a.rearrange("p (r c) -> p r c", c=w)

        everywhere = lambda a: bass.AP(a.tensor, 0, [[0, TOK], [1, 1]])
        consts = ((w1t_s[0:HC + 1, 0, :], w1t[0:HC + 1]), (w1t_s[0:HC, 1, :], w1t[HC + 1:C + 1]),
                  (w1n_s[:, :, :], w1n), (w2t_s[:, :, :], w2t),
                  (wvt_s[0:HC + 1, 0, :], wvt[0:HC + 1]), (wvt_s[0:HC, 1, :], wvt[HC + 1:C + 1]),
                  (vt_s[0:HC + 1, 0, :], vt[0:HC + 1]), (vt_s[0:HC, 1, :], vt[HC + 1:C + 1]),
                  (qk_s[:, :, :], qk), (pt_s[:, :, :], pt),
                  (cols[0:TOK, 16:17], everywhere(alpha)), (cols[0:TOK, 17:18], everywhere(beta)),
                  (cols[0:HC, 2:4], b2), (cols[0:HC, 4:6], pb), (cols[:, 6:7], qb[0:128]),
                  (cols[0:64, 7:8], qb[128:C]), (cols[:, 8:9], kb[0:128]), (cols[64:128, 9:10], kb[128:C]),
                  (cols[:, 10:12], qscale), (id_s[:, :], ident), (g_s[:, :], gmat), (hsum_s[:, :], hsum),
                  (hcol_s[:, :, :], hcol), (hmask_s[:, :, :], hmask), (fsel_s[:, :], fsel), (cmask_s[:, :], cmask),
                  (tie_s[:, :], tie))
        CONSTS = 16 * len(consts)

        s_const = Signal("consts_loaded", 0)
        s_init = Signal("fills_done", 0)
        s_rows = Signal("bias_rows_filled", 0)
        s_fill = Signal("mask_filled", 0)
        s_scat = Signal("bias_scattered", 0)
        s_mask = Signal("mask_loaded", 0)
        s_sbias = Signal("query_bias_scaled", 0)
        s_neg = Signal("alpha_beta_negated", 0)
        s_x = [Signal(f"image_loaded_in_{n}", 16, once=32 - 16 * n) for n in range(2)]
        s_st = Signal("bands_stored", 16 * NBAND)
        s_pool = Signal("pool_sums_ready", 2)
        s_sum = Signal("channel_sums_ready", 2)
        s_nmean = Signal("minus_means_ready", 2)
        s_sq = Signal("square_sums_ready", 4 * PIECES)
        s_vred = Signal("variances_ready", 2)
        s_veps = Signal("variance_eps_ready", 2)
        s_rstd = Signal("rstd_ready", 2)
        s_nmr = Signal("shift_ready", 3)
        s_pooled = Signal("pooled_ready", 1)
        s_cent = Signal("centres_copied", 1)
        s_csq = Signal("centre_squares_ready", 1)
        s_cn2 = Signal("centre_norms2_copied", 1)
        s_crt = Signal("centre_norms_ready", 1)
        s_cchain = Signal("centre_steps", 3)
        s_cbd = Signal("centres_spread", 1)
        s_xtok = Signal("chunk_normalised", TT)
        s_nd = Signal("token_norms2_copied", TT)
        s_nrt = Signal("token_norms_ready", TT)
        s_rn = Signal("token_norm_steps", 2 * TT)
        s_z = Signal("cosines_ready", TT)
        s_e = Signal("sigmoid_exp_ready", TT)
        s_chain = Signal("argmax_steps", 7 * TT)
        s_won = Signal("similarities_masked", TT)
        s_rc = Signal("count_steps", 2)
        s_ys = Signal("cluster_sums_scaled", 1)
        s_xband = Signal("band_normalised", NBAND)
        s_patch = Signal("key_patches_ready", STRIPS)
        s_begun = {e: Signal(f"step_begun_by_{e}", 0) for e in ("dve", "pool")}
        s_scores = Signal("scores_ready", STEPS)
        s_max = Signal("maxima_ready", STEPS)
        s_exp = Signal("probabilities_ready", STEPS)
        s_tr = Signal("probabilities_transposed", STEPS)
        s_trs = Signal("probabilities_transposed_copied", STEPS)
        s_av = Signal("attention_ready", NBAND * PAIRS)
        s_rec = Signal("denominators_inverted", NBAND * PAIRS)
        s_on = Signal("attention_normalised", NBAND * PAIRS)
        count = lambda turn, e=None: sum(j[0] == turn and e in (None, emptier(j)) for j in ORDERED)
        s_job = [Signal(f"side_jobs{t}_filled", count(t)) for t in range(2)]
        s_emp = {(t, e): Signal(f"side_jobs{t}_emptied_by_{e}", count(t, e), once=1) for t in range(2) for e in ("act", "dve")}

        finished = {}
        for g in range(NBAND * PAIRS):
            last_unit = NBAND * (g % PAIRS) + NBAND - 1
            finished.setdefault(DUOS * (g // PAIRS) + last_unit // 2, []).append(g)

        def units(d):
            b, j = divmod(d, DUOS)
            return [(b, u % NBAND, ORDER[u // NBAND]) for u in range(2 * j, min(2 * j + 2, UNITS))]

        def chunk(slot, phase):
            n, r = divmod(slot - CHUNK0 - phase, PERIOD)
            return n if r == 0 and 0 <= n < TT else None

        def images(engine, turn):
            turn(0, 1, (1,))
            with engine.Fori(0, B // 2 - 1) as two:
                turn(two * 2, 0, (0, 1))
                turn(two * 2 + 1, 1, (0, 1))
            turn(B - 2, 0, (0, 1))
            turn(B - 1, 1, (0,))

        block = ctx.enter_context(nc.Block())

        @block.sync
        def _(sp):
            def load(img, n):
                for t in range(2):
                    sp.dma_start(xbuf[n][0:HC, t, :], x[bass.ds(img, 1), t * HC:(t + 1) * HC, :].rearrange("o p n -> (o p) n"))\
                        .then_inc(s_x[n].sem, 16)

            for dst, src in consts:
                sp.dma_start(dst, src).then_inc(s_const.sem, 16)
            load(0, 0)
            load(1, 1)

            def store(img, n):
                for b in range(NBAND):
                    sp.wait_ge(s_emp[0, "dve"].sem, s_emp[0, "dve"].at(img, NTH_BY[0, "proj", b, 1]))
                    sp.dma_start(out[bass.ds(img, 1), :, b * BAND:(b + 1) * BAND].rearrange("o (t p) n -> (o p) t n", p=HC),
                                 xbuf[n][0:HC, :, b * BAND:(b + 1) * BAND]).then_inc(s_st.sem, 16)

            with sp.Fori(0, B // 2 - 1) as two:
                for n in range(2):
                    store(two * 2 + n, n)
                    sp.wait_ge(s_st.sem, s_st.at(two * 2 + n, 16 * NBAND))
                    load(two * 2 + (n + 2), n)
            store(B - 2, 0)
            store(B - 1, 1)
            sp.wait_ge(s_st.sem, 16 * NBAND * B)

        @block.gpsimd
        def _(pool):
            nc.gpsimd.memset(kpad[:, :, :], 0.0).then_inc(s_init.sem, 1)
            nc.gpsimd.memset(patch[:, :, :, :, :], 0.0).then_inc(s_init.sem, 1)
            nc.gpsimd.memset(prob[:, :, :, :], 0.0).then_inc(s_init.sem, 1)
            nc.gpsimd.memset(vring[:, :, :, :], 1.0).then_inc(s_init.sem, 1)
            nc.gpsimd.memset(halfs[:, :], 0.5).then_inc(s_init.sem, 1)
            nc.gpsimd.memset(nhalf[:, :], -0.5).then_inc(s_init.sem, 1)
            nc.gpsimd.memset(ones[:, :], 1.0).then_inc(s_init.sem, 1)
            nc.gpsimd.memset(bmask[:, :, :], NEG).then_inc(s_fill.sem, 1)
            pool.wait_ge(s_fill.sem, 1)
            row = PAIRS * NK
            pool.dma_start(scratch.rearrange("(p n) -> p n", n=row), bmask[:, :, :].rearrange("p a n -> p (a n)"))\
                .then_inc(s_scat.sem, 16)
            pool.wait_ge(s_scat.sem, 16)
            for par in range(2):
                for pair in range(PAIRS):
                    for r in range(QB):
                        first = (par * 64 + r * QB) * row + pair * NK + r * KB
                        dst = bass.AP(scratch.tensor, first, [[row + 1, QB], [KB, WIN], [1, WIN]])
                        src = bass.AP(table.tensor, (2 * pair + par) * WIN * WIN, [[0, QB], [WIN, WIN], [1, WIN]])
                        pool.dma_start(dst, src).then_inc(s_scat.sem, 16)
            pool.wait_ge(s_scat.sem, 16 * (1 + 2 * PAIRS * QB))
            pool.dma_start(bmask[:, :, :].rearrange("p a n -> p (a n)"), scratch.rearrange("(p n) -> p n", n=row))\
                .then_inc(s_mask.sem, 16)
            pool.wait_ge(s_rows.sem, 5)

            def fill(img, xb, turn, s):
                if s >= 2:
                    old = NTH[(0 if s - 2 >= 2 else 1), "v", s - 2, 3]
                    old_turn = 0 if s - 2 >= 2 else 1
                    pool.wait_ge(s_job[old_turn].sem, s_job[old_turn].at(img, old))
                else:
                    pool.wait_ge(s_nmr.sem, s_nmr.at(img, 3))
                pool.sem_inc(s_begun["pool"].sem, 1)
                top, bottom = max(0, PAD - QB * s), min(QB, H + PAD - QB * s)
                v = patch[:, s % 2, :, :, :].rearrange("p t n (r c) -> p t n r c", c=KB)
                for r0, r1 in ((0, top), (bottom, QB)):
                    for t in range(2):
                        if r0 < r1:
                            nc.gpsimd.memset(v[:, t, :, r0:r1, :].rearrange("p n r c -> p n (r c)"), 0.0)
                for t in range(2):
                    for n0, n1, c0, c1 in ((0, 1, PAD, KB), (1, NBAND - 1, 0, KB), (NBAND - 1, NBAND, 0, KB - PAD)):
                        src = bass.AP(xb, t * NPIX + (QB * s - PAD + top) * W + QB * n0 - PAD + c0,
                                      [[2 * NPIX, HC + 1], [QB, n1 - n0], [W, bottom - top], [1, c1 - c0]])
                        last = nc.gpsimd.tensor_scalar(v[:, t, n0:n1, top:bottom, c0:c1], src,
                                                       rstd[:, 1, t:t + 1], nmr[:, 1, t:t + 1], ALU.mult, ALU.add)
                last.then_inc(s_patch.sem, 1)

            def turn(img, n, turns):
                nxt = img + 1 if 0 in turns else img
                xb = xbuf[n] if 0 in turns else None
                xn = xbuf[1 - n]
                for slot in range(SLOTS):
                    b, j = divmod(slot, DUOS)
                    if 0 in turns and j == 1 and b + 2 < STRIPS:
                        fill(img, xb, 0, b + 2)
                    if 1 not in turns:
                        continue
                    for g, at in ((0, 11), (1, STAT1 + 5)):
                        if slot == at:
                            pool.wait_ge(s_veps.sem, s_veps.at(nxt, g + 1))
                            nc.gpsimd.tensor_tensor(rstd[0:HC, g, :], veps[:, g, :], nhalf[0:HC, :], ALU.pow)\
                                .then_inc(s_rstd.sem, 1)
                    if slot == 15:
                        pool.wait_ge(s_cn2.sem, s_cn2.at(nxt, 1))
                        nc.gpsimd.tensor_tensor(cnrm[:, :], cn2[:, :], halfs[:, :], ALU.pow).then_inc(s_crt.sem, 1)
                    if (c := chunk(slot, 4)) is not None:
                        pool.wait_ge(s_nd.sem, s_nd.at(nxt, c + 1))
                        nc.gpsimd.tensor_tensor(rn[:, :], nd[:, 0:32], halfs[0:TOK, :], ALU.pow).then_inc(s_nrt.sem, 1)
                    if slot == HEAD1:
                        fill(nxt, xn, 1, 0)
                        fill(nxt, xn, 1, 1)

            images(pool, turn)

        @block.scalar
        def _(act):
            act.wait_ge(s_const.sem, CONSTS)
            act.wait_ge(s_init.sem, 7)
            for t in range(2):
                act.sem_inc(s_emp[t, "act"].sem, 1)
            for t, p in ((0, 128), (1, 64)):
                for e in range(2):
                    nc.scalar.activation(SBIAS[t][e][0:p], QBIAS(t)[0:p], ACT.Identity, bias=0.0,
                                         scale=SCALE[e][0:p]).then_inc(s_sbias.sem, 1)
            act.wait_ge(s_sbias.sem, 4)
            act.wait_ge(s_neg.sem, 1)

            def squares(nxt, xn, g, t):
                act.wait_ge(s_nmean.sem, s_nmean.at(nxt, g + 1))
                for k in range(PIECES):
                    done = PIECES * (2 * g + t) + k
                    if done:
                        act.wait_ge(s_sq.sem, s_sq.at(nxt, done))
                    nc.scalar.activation(junk[:, :], xn[0:HC, t, PIECE * k:PIECE * k + PIECE], ACT.Square,
                                         bias=nmean[:, t:t + 1], scale=1.0, accum_out=ssq[:, PIECES * t + k:PIECES * t + k + 1])\
                        .then_inc(s_sq.sem, 1)

            def empty(img, job):
                turn, kind, b = job[0:3]
                act.wait_ge(s_job[turn].sem, s_job[turn].at(img, NTH[job]))
                ps = psX[BANK[job]]
                if kind == "qk":
                    half, p = (0, 128) if job[3] == 0 else (1, 64)
                    for e in range(2):
                        dst = qbd[0:p, b % 3, half, :, 64 * e:64 * e + 64].rearrange("p n (r c) -> p n r c", c=QB)
                        last = nc.scalar.activation(dst, ps[0:p, 0:BAND].rearrange("p (r n c) -> p n r c", n=NBAND, c=QB),
                                                    ACT.Identity, bias=SBIAS[half][e][0:p], scale=SCALE[e][0:p])
                    if half:
                        dst = rows(kpad[0:64, 1, :], WP)[:, PAD + QB * b:PAD + QB * b + QB, PAD:PAD + W]
                        last = nc.scalar.activation(dst, rows(ps[64:128, 0:BAND]), ACT.Identity, bias=KBIAS(1)[64:128], scale=1.0)
                elif kind == "o":
                    c0, n4 = (0, 4) if job[3] == 0 else (4, 3)
                    for e in range(2):
                        src = ps[0:HC, 0:128 * n4].rearrange("p (n e r c) -> p e n r c", n=n4, e=2, c=QB)[:, e]
                        dst = ochan[:, e, :].rearrange("p (r n c) -> p n r c", n=NBAND, c=QB)[:, c0:c0 + n4]
                        last = nc.scalar.activation(dst, src, ACT.Copy)
                elif kind == "feat":
                    last = nc.scalar.activation(sq[:, job[3], :], ps[:, 0:BAND], ACT.Square)
                elif kind == "tok":
                    last = nc.scalar.activation(xT[:, 2 * job[3]:2 * job[3] + 2, :].rearrange("p a n -> p (a n)"),
                                                ps[0:TOK, 0:2 * (C + 1)], ACT.Copy)
                last.then_inc(s_emp[turn, "act"].sem, 1)

            def turn(img, n, turns):
                nxt = img + 1 if 0 in turns else img
                xn = xbuf[1 - n]
                for slot in range(SLOTS):
                    if 0 in turns and slot < STEPS:
                        act.wait_ge(s_max.sem, s_max.at(img, slot + 1))
                        if slot >= 3:
                            act.wait_ge(s_tr.sem, s_tr.at(img, slot - 2))
                        for j in range(len(units(slot))):
                            last = nc.scalar.activation(prob[:, slot % 3, j, 0:NK], msc[:, slot % 2, j, :], ACT.Exp,
                                                        bias=nmx[:, slot % 2, j:j + 1], scale=-1.0)
                        last.then_inc(s_exp.sem, 1)
                    d = slot - 2
                    if 0 in turns and 0 <= d < STEPS:
                        m = 256 * len(units(d))
                        act.wait_ge(s_tr.sem, s_tr.at(img, d + 1))
                        nc.scalar.activation(probT[:, d % 2, 0:m], psT[d % 2][0:KA, 0:m], ACT.Copy).then_inc(s_trs.sem, 1)
                    for job in JOBS[slot]:
                        if job[0] in turns and emptier(job) == "act":
                            empty(nxt if job[0] else img, job)
                    if 1 not in turns:
                        continue
                    for g, at in ((0, 8), (1, STAT1 + 2)):
                        for t in range(2):
                            if slot == at + t:
                                squares(nxt, xn, g, t)
                    if (c := chunk(slot, 6)) is not None:
                        act.wait_ge(s_z.sem, s_z.at(nxt, c + 1))
                        nc.scalar.activation(ee[:, :], zz[:, :], ACT.Exp, bias=NBETA, scale=NA).then_inc(s_e.sem, 1)

            images(act, turn)

        @block.vector
        def _(dve):
            dve.wait_ge(s_const.sem, CONSTS)
            dve.wait_ge(s_init.sem, 7)
            dve.wait_ge(s_mask.sem, 16)
            for t in range(2):
                dve.sem_inc(s_emp[t, "dve"].sem, 1)
            for a, v in ((xbuf[0][HC:HC + 1, :, :], 1.0), (xbuf[1][HC:HC + 1, :, :], 1.0), (pooled[HC:HC + 1, 0, :], 1.0),
                         (rstd[HC:HC + 1, :, :], 1.0), (nmr[HC:HC + 1, :, :], 0.0)):
                nc.vector.memset(a, v).then_inc(s_rows.sem, 1)
            nc.vector.tensor_scalar(cols[0:TOK, 0:2], cols[0:TOK, 16:18], -1.0, None, ALU.mult).then_inc(s_neg.sem, 1)
            dve.wait_ge(s_rows.sem, 5)

            def shift(nxt, g):
                dve.wait_ge(s_rstd.sem, s_rstd.at(nxt, g + 1))
                nc.vector.tensor_tensor(nmr[0:HC, g, :], nmean[:, :], rstd[0:HC, g, :], ALU.mult).then_inc(s_nmr.sem, 1)

            def normal_band(img, xb, b):
                for t in range(2):
                    last = nc.vector.tensor_scalar(xband[:, b % 2, t, :], xb[0:HC, t, BAND * b:BAND * b + BAND],
                                                   rstd[0:HC, 1, t:t + 1], nmr[0:HC, 1, t:t + 1], ALU.mult, ALU.add)
                last.then_inc(s_xband.sem, 1)

            def empty(img, xb, xn, job):
                turn, kind = job[0:2]
                dve.wait_ge(s_job[turn].sem, s_job[turn].at(img, NTH[job]))
                ps = psX[BANK[job]]
                if kind == "qk":
                    b = job[2]
                    dst = rows(kpad[:, 0, :], WP)[:, PAD + QB * b:PAD + QB * b + QB, PAD:PAD + W]
                    last = nc.vector.tensor_scalar(dst, rows(ps[:, 0:BAND]), KBIAS(0), None, ALU.add)
                elif kind == "v":
                    b, c0 = job[2], 2 * job[3]
                    m = min(2, NBAND - c0)
                    dst = vring[:, b % 3, c0:c0 + m, :].rearrange("p n (a w) -> p (n a) w", w=VW)
                    src = ps[0:KA, 0:m * C].rearrange("p (a e c) -> p a e c", e=2, c=DH)
                    for e in range(2):
                        last = nc.vector.tensor_copy(dst[:, :, (DH + 1) * e:(DH + 1) * e + DH], src[:, :, e, :])
                elif kind == "proj":
                    b, t = job[2:]
                    pix = xb[0:HC, t, b * BAND:(b + 1) * BAND]
                    last = nc.vector.scalar_tensor_tensor(pix, ps[0:HC, 0:BAND], PB[t], pix, ALU.add, ALU.add)
                elif kind == "mean":
                    last = nc.vector.tensor_scalar(nmean[:, :], ps[0:HC, 0:2], -1.0, None, ALU.mult)
                    last.then_inc(s_nmean.sem, 1)
                    last = nc.vector.memset(rcnt[0:1, 1:2], 0.0)
                elif kind == "var":
                    g = job[2]
                    nc.vector.tensor_reduce(veps[:, g, :], ps[0:HC, 0:2 * PIECES].rearrange("p (t k) -> p t k", t=2),
                                            AX.X, ALU.add).then_inc(s_vred.sem, 1)
                    dve.wait_ge(s_vred.sem, s_vred.at(img, g + 1))
                    nc.vector.tensor_scalar(veps[:, g, :], veps[:, g, :], EPS, None, ALU.add).then_inc(s_veps.sem, 1)
                    last = nc.vector.memset(rcnt[0:1, 1:2], 0.0)
                elif kind == "centres":
                    nc.vector.tensor_copy(cent[:, :], ps[:, 0:32]).then_inc(s_cent.sem, 1)
                    last = nc.vector.tensor_copy(pooledT[:, :], ps[0:16, 64:64 + C + 1])
                elif kind == "norms":
                    nc.vector.tensor_copy(cn2[:, :], ps[:, 0:32]).then_inc(s_cn2.sem, 1)
                    last = nc.vector.memset(rcnt[0:1, 1:2], 0.0)
                elif kind == "pixels":
                    for t in range(2):
                        src = ps[0:KP[t], 128 * t:128 * t + 128].rearrange("p (m f n) -> p m f n", m=2, f=4)
                        last = nc.vector.tensor_copy(qsim[0:KP[t], t, :, :].rearrange("p f (m n) -> p m f n", m=2), src)
                elif kind == "dots":
                    nc.vector.tensor_copy(nd[:, :], ps[0:TOK, 0:160]).then_inc(s_nd.sem, 1)
                    last = nc.vector.memset(rcnt[0:1, 1:2], 0.0)
                elif kind == "sums":
                    c = job[2]
                    if c == 0:
                        nc.vector.tensor_copy(yacc[:, :], ps[:, 0:C + 2])
                    else:
                        nc.vector.tensor_tensor(yacc[:, :], ps[:, 0:C + 2], yacc[:, :], ALU.add)
                    last = nc.vector.tensor_copy(simT[:, TOK * c:TOK * c + TOK], ps[:, 256:256 + TOK])
                elif kind == "sumsT":
                    nc.vector.tensor_copy(ysT[0:HC + 1, 0, :], ps[0:HC + 1, 0:128])
                    last = nc.vector.tensor_copy(ysT[0:HC, 1, :], ps[0:HC, 128:256])
                elif kind == "agg":
                    last = nc.vector.tensor_tensor(agg[:, :, :].rearrange("p m n -> p (m n)"), ps[:, 0:256],
                                                   hmask_s[:, :, :].rearrange("p m n -> p (m n)"), ALU.mult)
                elif kind == "gout":
                    last = nc.vector.tensor_copy(gout[:, :], ps[:, 0:C])
                elif kind == "out0":
                    f, hf, t = job[2] // 4, job[2] // 2 % 2, job[2] % 2
                    nr = 16 if hf == 0 else 12
                    r0, c0 = FOLD * (f // 2) + 16 * hf, FOLD * (f % 2)
                    pix = rows(xn[0:HC, t, :])[:, r0:r0 + nr, c0:c0 + FOLD]
                    last = nc.vector.scalar_tensor_tensor(pix, rows(ps[0:HC, 0:nr * FOLD], FOLD), B2[t], pix, ALU.add, ALU.add,
                                                          accum_out=osum[:, t, job[2] // 2:job[2] // 2 + 1])
                last.then_inc(s_emp[turn, "dve"].sem, 1)

            def turn(img, n, turns):
                nxt = img + 1 if 0 in turns else img
                xb, xn = xbuf[n], xbuf[1 - n]
                for slot in range(SLOTS):
                    b, j = divmod(slot, DUOS)
                    if 0 in turns and slot < STEPS:
                        dve.wait_ge(s_scores.sem, s_scores.at(img, slot + 1))
                        if slot >= 2:
                            dve.wait_ge(s_exp.sem, s_exp.at(img, slot - 1))
                        dve.sem_inc(s_begun["dve"].sem, 1)
                        for k, (_, _, pair) in enumerate(units(slot)):
                            last = nc.vector.tensor_tensor_reduce(
                                out=msc[:, slot % 2, k, :], in0=psS[slot % 2][:, k * NK:(k + 1) * NK], in1=bmask[:, pair, :],
                                scale=-1.0, scalar=3.0e38, op0=ALU.add, op1=ALU.min, accum_out=nmx[:, slot % 2, k:k + 1])
                        last.then_inc(s_max.sem, 1)
                    if 0 in turns and j == 0 and b + 2 < NBAND:
                        normal_band(img, xb, b + 2)
                    for g in finished.get(slot - 4, []) if 0 in turns else ():
                        dve.wait_ge(s_av.sem, s_av.at(img, g + 1))
                        v = psO[g % 2][:, 0:NBAND * VW].rearrange("p (n w) -> p n w", w=VW)
                        nc.vector.reciprocal(orec[:, g % 2, :], v[:, :, DH]).then_inc(s_rec.sem, 1)
                        dve.wait_ge(s_rec.sem, s_rec.at(img, g + 1))
                        pair = ORDER[g % PAIRS]
                        for e in range(2):
                            q = slice(64 * e, 64 * e + 64)
                            last = nc.vector.tensor_tensor(
                                otok[q, :, DH * pair:DH * pair + DH], v[q, :, (DH + 1) * e:(DH + 1) * e + DH],
                                orec[q, g % 2, :, None].broadcast_to([64, NBAND, DH]), ALU.mult)
                        last.then_inc(s_on.sem, 1)
                    for job in JOBS[slot]:
                        if job[0] in turns and emptier(job) == "dve":
                            empty(nxt if job[0] else img, xb, xn, job)
                    if 1 not in turns:
                        continue
                    for t in range(2):
                        if slot == 5 + t:
                            if t == 0:
                                dve.wait_ge(s_x[1 - n].sem, s_x[1 - n].at(nxt, 0))
                            v = xn[0:HC, t, :].rearrange("p (a r b c) -> p a b r c", a=4, b=4, c=POOL)
                            nc.vector.tensor_reduce(psums[:, t, :].rearrange("p (a b) -> p a b", b=4), v, AX.XY, ALU.add)\
                                .then_inc(s_pool.sem, 1)
                    if slot == 6:
                        dve.wait_ge(s_pool.sem, s_pool.at(nxt, 2))
                        nc.vector.tensor_reduce(ssum[:, :], psums[:, :, :], AX.X, ALU.add).then_inc(s_sum.sem, 1)
                    if slot == 12:
                        shift(nxt, 0)
                        nc.vector.tensor_scalar(r196[:, :], rstd[0:HC, 0, :], 1.0 / (POOL * POOL), None, ALU.mult)\
                            .then_inc(s_nmr.sem, 1)
                        dve.wait_ge(s_nmr.sem, s_nmr.at(nxt, 2))
                        for t in range(2):
                            last = nc.vector.tensor_scalar(pooled[0:HC, t, :], psums[:, t, :], r196[:, t:t + 1],
                                                           nmr[0:HC, 0, t:t + 1], ALU.mult, ALU.add)
                        last.then_inc(s_pooled.sem, 1)
                    if slot == 13:
                        dve.wait_ge(s_cent.sem, s_cent.at(nxt, 1))
                        nc.vector.tensor_tensor(csq[:, :], cent[:, :], cent[:, :], ALU.mult).then_inc(s_csq.sem, 1)
                    if slot == 16:
                        dve.wait_ge(s_crt.sem, s_crt.at(nxt, 1))
                        nc.vector.tensor_scalar(cn2[:, :], cnrm[:, :], 1e-12, None, ALU.max).then_inc(s_cchain.sem, 1)
                        dve.wait_ge(s_cchain.sem, s_cchain.at(nxt, 1))
                        nc.vector.reciprocal(csq[:, :], cn2[:, :]).then_inc(s_cchain.sem, 1)
                        dve.wait_ge(s_cchain.sem, s_cchain.at(nxt, 2))
                        nc.vector.tensor_tensor(cn[:, :, :].rearrange("p m n -> p (m n)"), cent[:, :], csq[:, :], ALU.mult)\
                            .then_inc(s_cchain.sem, 1)
                        dve.wait_ge(s_cchain.sem, s_cchain.at(nxt, 3))
                        for m in range(2):
                            for f in range(4):
                                src = cn[:, m, :].rearrange("p (a u b v) -> p a b u v", a=2, u=2, b=2)[:, f // 2, f % 2]
                                src = src[:, None, :, :].broadcast_to([128, 4, 2, 2])
                                last = nc.vector.tensor_tensor(cbd[:, m, 16 * f:16 * f + 16].rearrange("p (h u v) -> p h u v", h=4, u=2),
                                                               src, cmask_s[:, :].rearrange("p (h u v) -> p h u v", h=4, u=2), ALU.mult)
                        last.then_inc(s_cbd.sem, 1)
                    if (c := chunk(slot, 0)) is not None:
                        for t in range(2):
                            for fh in range(2):
                                src = rows(xn[:, t, :])[:, FOLD * fh + TR * c:FOLD * fh + TR * c + TR, :]
                                dst = xtok[:, c % 2, t, 2 * TOK * fh:2 * TOK * fh + 2 * TOK]
                                last = nc.vector.tensor_scalar(dst.rearrange("p (f r c) -> p f r c", f=2, r=TR),
                                                               src.rearrange("p r (f c) -> p f r c", f=2),
                                                               rstd[:, 0, t:t + 1], nmr[:, 0, t:t + 1], ALU.mult, ALU.add)
                        last.then_inc(s_xtok.sem, 1)
                    by4 = lambda a: a[:, :].rearrange("p (n m) -> p n m", m=4)
                    if (c := chunk(slot, 5)) is not None:
                        dve.wait_ge(s_nrt.sem, s_nrt.at(nxt, c + 1))
                        nc.vector.tensor_scalar(rm[:, :], rn[:, :], 1e-12, None, ALU.max).then_inc(s_rn.sem, 1)
                        dve.wait_ge(s_rn.sem, s_rn.at(nxt, 2 * c + 1))
                        nc.vector.reciprocal(mx[:, :], rm[:, :]).then_inc(s_rn.sem, 1)
                        dve.wait_ge(s_rn.sem, s_rn.at(nxt, 2 * c + 2))
                        nc.vector.tensor_tensor(by4(zz), nd[:, 32:160].rearrange("p (n m) -> p n m", m=4),
                                                mx[:, :, None].broadcast_to([TOK, 32, 4]), ALU.mult).then_inc(s_z.sem, 1)
                    if (c := chunk(slot, 7)) is not None:
                        k = 7 * c
                        top = mx[:, :, None].broadcast_to([TOK, 32, 4])
                        dve.wait_ge(s_e.sem, s_e.at(nxt, c + 1))
                        nc.vector.tensor_scalar(key[:, :], ee[:, :], 1.0, None, ALU.add).then_inc(s_chain.sem, 1)
                        dve.wait_ge(s_chain.sem, s_chain.at(nxt, k + 1))
                        nc.vector.reciprocal(sim[:, :], key[:, :]).then_inc(s_chain.sem, 1)
                        dve.wait_ge(s_chain.sem, s_chain.at(nxt, k + 2))
                        nc.vector.tensor_reduce(mx[:, :], by4(sim), AX.X, ALU.max).then_inc(s_chain.sem, 1)
                        dve.wait_ge(s_chain.sem, s_chain.at(nxt, k + 3))
                        nc.vector.tensor_tensor(by4(key), by4(sim), top, ALU.is_equal).then_inc(s_chain.sem, 1)
                        dve.wait_ge(s_chain.sem, s_chain.at(nxt, k + 4))
                        nc.vector.tensor_tensor(by4(won), by4(key), tie_s[:, None, :].broadcast_to([TOK, 32, 4]), ALU.mult)\
                            .then_inc(s_chain.sem, 1)
                        dve.wait_ge(s_chain.sem, s_chain.at(nxt, k + 5))
                        nc.vector.tensor_reduce(mx[:, :], by4(won), AX.X, ALU.max).then_inc(s_chain.sem, 1)
                        dve.wait_ge(s_chain.sem, s_chain.at(nxt, k + 6))
                        nc.vector.tensor_tensor(by4(key), by4(won), top, ALU.is_equal).then_inc(s_chain.sem, 1)
                        dve.wait_ge(s_chain.sem, s_chain.at(nxt, k + 7))
                        nc.vector.tensor_tensor(won[:, :], sim[:, :], key[:, :], ALU.mult).then_inc(s_won.sem, 1)
                    if slot == END0:
                        dve.wait_ge(s_emp[1, "dve"].sem, s_emp[1, "dve"].at(nxt, NTH_BY[1, "sums", TT - 1]))
                        nc.vector.tensor_scalar(rcnt[:, 0:1], yacc[:, C + 1:C + 2], 1.0, None, ALU.add).then_inc(s_rc.sem, 1)
                        dve.wait_ge(s_rc.sem, s_rc.at(nxt, 1))
                        nc.vector.reciprocal(rcnt[:, 0:1], rcnt[:, 0:1]).then_inc(s_rc.sem, 1)
                        dve.wait_ge(s_rc.sem, s_rc.at(nxt, 2))
                        nc.vector.tensor_scalar(ys[:, :], yacc[:, 0:C + 1], rcnt[:, 0:1], None, ALU.mult).then_inc(s_ys.sem, 1)
                    if slot == STAT1:
                        dve.wait_ge(s_emp[1, "dve"].sem, s_emp[1, "dve"].at(nxt, NTH_BY[1, "out0", 15]))
                        nc.vector.tensor_reduce(ssum[:, :], osum[:, :, :], AX.X, ALU.add).then_inc(s_sum.sem, 1)
                    if slot == STAT1 + 6:
                        shift(nxt, 1)
                        dve.wait_ge(s_nmr.sem, s_nmr.at(nxt, 3))
                        for b in range(2):
                            normal_band(nxt, xn, b)

            images(dve, turn)

        @block.tensor
        def _(pe):
            mm, mm_t = nc.tensor.matmul, nc.tensor.transpose
            pe.wait_ge(s_const.sem, CONSTS)
            pe.wait_ge(s_init.sem, 7)
            pe.wait_ge(s_rows.sem, 5)

            def wait_emptied(img, nxt, job):
                s = s_emp[job[0], emptier(job)]
                pe.wait_ge(s.sem, s.at(nxt if job[0] else img, NTH_BY[job]))

            def fill(img, nxt, job, turns):
                turn, kind = job[0:2]
                own = nxt if turn else img
                had = before(job, turns)
                if had:
                    wait_emptied(img, nxt, had)
                ps = psX[BANK[job]]
                if kind == "qk":
                    b, k = job[2:]
                    pe.wait_ge(s_xband.sem, s_xband.at(own, b + 1))
                    for t in range(2):
                        last = mm(ps[:, 0:BAND], qk_s[:, t, 128 * k:128 * k + 128], xband[:, b % 2, t, :], start=(t == 0), stop=(t == 1))
                elif kind == "v":
                    b = job[2]
                    pe.wait_ge(s_patch.sem, s_patch.at(own, b + 1))
                    for c in range(2 * job[3], min(2 * job[3] + 2, NBAND)):
                        o = C * (c % 2)
                        for t in range(2):
                            last = mm(ps[0:KA, o:o + C], patch[0:KP[t], b % 2, t, c, :], vt_s[0:KP[t], t, :],
                                      start=(t == 0), stop=(t == 1))
                elif kind == "o":
                    b = job[2]
                    c0, n4 = (0, 4) if job[3] == 0 else (4, 3)
                    pe.wait_ge(s_on.sem, s_on.at(own, PAIRS * (b + 1)))
                    for k in range(n4):
                        last = mm_t(ps[0:HC, 128 * k:128 * k + 128], otok[:, c0 + k, :], id_s[:, :])
                elif kind == "proj":
                    b, t = job[2:]
                    wait_emptied(img, nxt, (0, "o", b, 1))
                    for e in range(2):
                        last = mm(ps[0:HC, 0:BAND], pt_s[:, e, HC * t:HC * t + HC], ochan[:, e, :], start=(e == 0), stop=(e == 1))
                elif kind == "mean":
                    pe.wait_ge(s_sum.sem, s_sum.at(own, job[2] + 1))
                    last = mm(ps[0:HC, 0:2], g_s[:, :], ssum[:, :], start=True, stop=True)
                elif kind == "var":
                    pe.wait_ge(s_sq.sem, s_sq.at(own, 2 * PIECES * (job[2] + 1)))
                    last = mm(ps[0:HC, 0:2 * PIECES], g_s[:, :], ssq[:, :], start=True, stop=True)
                elif kind == "centres":
                    pe.wait_ge(s_pooled.sem, s_pooled.at(own, 1))
                    for m in range(2):
                        for t in range(2):
                            mm(ps[:, 16 * m:16 * m + 16], w1t_s[0:KP[t], t, 128 * m:128 * m + 128],
                               pooled[0:KP[t], t, :], start=(t == 0), stop=(t == 1))
                    mm_t(ps[0:16, 64:64 + HC + 1], pooled[0:HC + 1, 0, :], id_s[0:HC + 1, 0:HC + 1])
                    last = mm_t(ps[0:16, 64 + HC + 1:64 + C + 1], pooled[0:HC, 1, :], id_s[0:HC, 0:HC])
                elif kind == "norms":
                    pe.wait_ge(s_csq.sem, s_csq.at(own, 1))
                    last = mm(ps[:, 0:32], hsum_s[:, :], csq[:, :], start=True, stop=True)
                elif kind == "pixels":
                    pe.wait_ge(s_cbd.sem, s_cbd.at(own, 1))
                    for t in range(2):
                        for m in range(2):
                            last = mm(ps[0:KP[t], 128 * t + 64 * m:128 * t + 64 * m + 64],
                                      w1n_s[:, m, (HC + 1) * t:(HC + 1) * t + KP[t]], cbd[:, m, :], start=True, stop=True)
                elif kind == "feat":
                    c, m = job[2:]
                    pe.wait_ge(s_xtok.sem, s_xtok.at(own, c + 1))
                    for t in range(2):
                        last = mm(ps[:, 0:BAND], w1t_s[0:KP[t], t, 128 * m:128 * m + 128], xtok[0:KP[t], c % 2, t, :],
                                  start=(t == 0), stop=(t == 1))
                elif kind == "tok":
                    c, h = job[2:]
                    for k in range(2):
                        o, q = (C + 1) * k, TOK * (2 * h + k)
                        mm_t(ps[0:TOK, o:o + HC + 1], xtok[0:HC + 1, c % 2, 0, q:q + TOK], id_s[0:HC + 1, 0:HC + 1])
                        last = mm_t(ps[0:TOK, o + HC + 1:o + C + 1], xtok[0:HC, c % 2, 1, q:q + TOK], id_s[0:HC, 0:HC])
                elif kind == "dots":
                    c = job[2]
                    wait_emptied(img, nxt, (1, "feat", c, 1))
                    wait_emptied(img, nxt, (1, "pixels"))
                    for f in range(4):
                        q = slice(TOK * f, TOK * f + TOK)
                        for m in range(2):
                            mm(ps[0:TOK, HEADS0 * f:HEADS0 * f + HEADS0], sq[:, m, q], hcol_s[:, m, :], start=(m == 0), stop=(m == 1))
                        for t in range(2):
                            last = mm(ps[0:TOK, 32 + HM * f:32 + HM * f + HM], xtok[0:KP[t], c % 2, t, q], qsim[0:KP[t], t, f, :],
                                      start=(t == 0), stop=(t == 1))
                elif kind == "sums":
                    c = job[2]
                    pe.wait_ge(s_won.sem, s_won.at(own, c + 1))
                    wait_emptied(img, nxt, (1, "tok", c, 1))
                    if c == 0:
                        wait_emptied(img, nxt, (1, "centres"))
                        mm(ps[:, 0:C + 1], fsel_s[:, :], pooledT[:, :], start=True, stop=False, skip_group_check=True)
                    for f in range(4):
                        q = slice(HM * f, HM * f + HM)
                        mm(ps[q, 0:C + 1], won[:, q], xT[:, f, :], start=(c > 0), stop=True, skip_group_check=True)
                    for f in range(4):
                        q = slice(HM * f, HM * f + HM)
                        mm(ps[q, C + 1:C + 2], key[:, q], ones[0:TOK, :], start=True, stop=True)
                    last = mm_t(ps[:, 256:256 + TOK], won[:, :], id_s[0:TOK, 0:TOK])
                elif kind == "sumsT":
                    pe.wait_ge(s_ys.sem, s_ys.at(own, 1))
                    mm_t(ps[0:HC + 1, 0:128], ys[:, 0:HC + 1], id_s[:, :])
                    last = mm_t(ps[0:HC, 128:256], ys[:, HC + 1:C + 1], id_s[:, :])
                elif kind == "agg":
                    wait_emptied(img, nxt, (1, "sumsT"))
                    for m in range(2):
                        for t in range(2):
                            last = mm(ps[:, 128 * m:128 * m + 128], wvt_s[0:KP[t], t, 128 * m:128 * m + 128],
                                      ysT[0:KP[t], t, :], start=(t == 0), stop=(t == 1))
                elif kind == "gout":
                    wait_emptied(img, nxt, (1, "agg"))
                    for m in range(2):
                        last = mm(ps[:, 0:C], agg[:, m, :], w2t_s[:, m, :], start=(m == 0), stop=(m == 1))
                elif kind == "out0":
                    wait_emptied(img, nxt, (1, "gout"))
                    f, hf, t = job[2] // 4, job[2] // 2 % 2, job[2] % 2
                    m = (4 if hf == 0 else 3) * TOK
                    q = slice(HM * f, HM * f + HM)
                    last = mm(ps[0:HC, 0:m], gout[q, HC * t:HC * t + HC], simT[q, 4 * TOK * hf:4 * TOK * hf + m],
                              start=True, stop=True)
                last.then_inc(s_job[turn].sem, 1)

            def turn(img, n, turns):
                nxt = img + 1 if 0 in turns else img
                for slot in range(SLOTS):
                    todo = [job for job in JOBS[slot] if job[0] in turns]
                    if 0 in turns and slot < STEPS:
                        if slot == 0:
                            for e in ("act", "dve"):
                                pe.wait_ge(s_emp[0, e].sem, s_emp[0, e].at(img, 0))
                                pe.wait_ge(s_emp[1, e].sem, s_emp[1, e].at(img, count(1, e)))
                        elif slot % DUOS == 0:
                            b = slot // DUOS
                            if 2 <= b + 1 < NBAND:
                                for k in (1, 2):
                                    wait_emptied(img, nxt, (0, "qk", b + 1, k))
                            if 2 <= b + 1:
                                wait_emptied(img, nxt, (0, "v", b + 1, 3))
                        if slot >= 2:
                            pe.wait_ge(s_max.sem, s_max.at(img, slot - 1))
                        for j, (b, c, pair) in enumerate(units(slot)):
                            half, p0 = pair // 2, 64 * (pair % 2)
                            keys = rows(kpad[p0:p0 + 64, half, :], WP)[:, QB * b:QB * b + KB, QB * c:QB * c + KB]
                            last = mm(psS[slot % 2][:, j * NK:(j + 1) * NK], qbd[p0:p0 + 64, b % 3, half, c, :], keys,
                                      start=True, stop=True)
                        last.then_inc(s_scores.sem, 1)
                    for job in todo[0:1]:
                        fill(img, nxt, job, turns)
                    d = slot - 2
                    if 0 in turns and 0 <= d < STEPS:
                        pe.wait_ge(s_exp.sem, s_exp.at(img, d + 1))
                        if d >= 2:
                            pe.wait_ge(s_trs.sem, s_trs.at(img, d - 1))
                        for j in range(len(units(d))):
                            for k in range(2):
                                last = mm_t(psT[d % 2][0:KA, 256 * j + 128 * k:256 * j + 128 * k + 128],
                                            prob[:, d % 3, j, KA * k:KA * k + KA], id_s[:, :])
                        last.then_inc(s_tr.sem, 1)
                    for job in todo[1:2]:
                        fill(img, nxt, job, turns)
                    d = slot - 3
                    if 0 in turns and 0 <= d < STEPS:
                        pe.wait_ge(s_trs.sem, s_trs.at(img, d + 1))
                        for j, (b, c, pair) in enumerate(units(d)):
                            g = PAIRS * b + ORDER.index(pair)
                            if c == 0 and g >= 2:
                                pe.wait_ge(s_on.sem, s_on.at(img, g - 1))
                            for k, p in enumerate((KA, KBB)):
                                last = mm(psO[g % 2][:, VW * c:VW * c + VW],
                                          probT[0:p, d % 2, 256 * j + 128 * k:256 * j + 128 * k + 128],
                                          vring[0:p, (b + k) % 3, c, VW * pair:VW * pair + VW], start=(k == 0), stop=(k == 1))
                            if c == NBAND - 1:
                                last.then_inc(s_av.sem, 1)
                    for job in todo[2:]:
                        fill(img, nxt, job, turns)

            images(pe, turn)


def kernel(x, L0_conv_W1, L0_conv_b1, L0_conv_Wv, L0_conv_bv, L0_conv_W2, L0_conv_b2, L0_conv_alpha, L0_conv_beta,
           L1_conv_qkv_w, L1_conv_qkv_b, L1_conv_proj_w, L1_conv_proj_b, L1_conv_bias_table):
    import numpy as np
    import concourse.bacc as bacc
    from concourse.bass_utils import run_bass_kernel_spmd

    def halves(wt):
        return np.ascontiguousarray(np.asarray(wt).reshape(2, HC, -1).transpose(1, 0, 2))

    def with_bias(wt, b):
        wt, b = np.asarray(wt), np.asarray(b)
        return np.concatenate([wt[:HC], b[None, :], wt[HC:]], 0)

    W1, W2, Wv, qkv, proj = (np.asarray(a) for a in (L0_conv_W1, L0_conv_W2, L0_conv_Wv, L1_conv_qkv_w, L1_conv_proj_w))
    qkv_b = np.asarray(L1_conv_qkv_b)
    w1n = np.concatenate([W1[:, :HC], np.asarray(L0_conv_b1)[:, None], W1[:, HC:]], 1)
    projT = proj.T.reshape(PAIRS, 2, DH, C).transpose(0, 2, 1, 3).reshape(HC, 2, C)
    f = np.float32
    p = np.arange(128)
    chan = np.arange(HC)
    gmat = ((chan[:, None] // GC) == (chan[None, :] // GC)).astype(f) / f(GC * NPIX)
    hsum = ((p[:, None] // 32) == (p[None, :] // 32)).astype(f)
    hcol = np.stack([((4 * m + p[:, None] // 32) == np.arange(HEADS0)[None, :]).astype(f) for m in range(2)], 1)
    fhm = np.arange(128)
    hmask = np.stack([((4 * m + p[:, None] // 32) == ((fhm % 32) // 4)[None, :]).astype(f) for m in range(2)], 1)
    rc = np.arange(16)
    R, Cc = rc // 4, rc % 4
    fold, cen = 2 * (R // 2) + Cc // 2, 2 * (R % 2) + Cc % 2
    fsel = ((fold[:, None] == (fhm // 32)[None, :]) & (cen[:, None] == (fhm % 4)[None, :])).astype(f)
    cmask = ((p[:, None] // 32) == (np.arange(16) // 4)[None, :]).astype(f)
    tie = np.broadcast_to(np.array([4, 3, 2, 1], f), (TOK, 4))
    qscale = np.stack([((p // 32) % 2 == e).astype(f) * f(DH ** -0.5) for e in range(2)], 1)
    arrays = {
        "x": np.asarray(x).reshape(B, C, NPIX),
        "w1t": with_bias(W1.T, L0_conv_b1), "w1n": w1n.reshape(2, 128, C + 1).transpose(1, 0, 2),
        "wvt": with_bias(Wv.T, L0_conv_bv), "w2t": W2.T.reshape(2, 128, C).transpose(1, 0, 2),
        "b2": np.asarray(L0_conv_b2).reshape(2, HC).T,
        "alpha": np.asarray(L0_conv_alpha).reshape(1, 1), "beta": np.asarray(L0_conv_beta).reshape(1, 1),
        "qk": halves(np.concatenate([qkv[:128], qkv[C:C + 128], qkv[128:C], qkv[C + 128:2 * C]], 0).T), "qb": qkv_b[:C, None], "kb": qkv_b[C:2 * C, None],
        "vt": with_bias(qkv[2 * C:].T, qkv_b[2 * C:]), "pt": projT,
        "pb": np.asarray(L1_conv_proj_b).reshape(2, HC).T, "table": np.asarray(L1_conv_bias_table).T,
        "ident": np.eye(128, dtype=f), "gmat": gmat, "hsum": hsum, "hcol": hcol, "hmask": hmask, "fsel": fsel,
        "cmask": cmask, "tie": tie, "qscale": qscale,
    }
    nc = bacc.Bacc("TRN2", target_bir_lowering=False, num_devices=1)
    ins = {}
    arrays = {f"in_{k}": np.ascontiguousarray(v) for k, v in arrays.items()}
    for k, v in arrays.items():
        ins[k[3:]] = nc.dram_tensor(k, v.shape, mybir.dt.from_np(v.dtype), kind="ExternalInput").ap()
    out = nc.dram_tensor("out_0", (B, C, NPIX), F32, kind="ExternalOutput").ap()
    scratch = nc.dram_tensor("mask_scratch", (128 * PAIRS * NK,), F32, kind="Internal").ap()
    build(nc, out=out, scratch=scratch, **ins)
    r = run_bass_kernel_spmd(nc, [arrays], core_ids=[0])
    return r.results[0]["out_0"].reshape(B, C, H, W)
```

```python
import concourse.bass as bass
from concourse import mybir
from contextlib import ExitStack

F32 = mybir.dt.float32
ALU = mybir.AluOpType
ACT = mybir.ActivationFunctionType
AX = mybir.AxisListType

B, C, H, W = 32, 192, 56, 56
HC = C // 2
NPIX = H * W
GROUPS = 32
GC = C // GROUPS
EPS = 1e-5
HEADS0, D0 = 8, 256
FOLD = 28
POOL = 14
TR = 4
TT = FOLD // TR
TOK = TR * FOLD
HM = HEADS0 * 4
HEADS1, DH, WIN = 6, 32, 7
PAD = WIN // 2
WP = W + 2 * PAD
QB = 8
KB = QB + 2 * PAD
NK = KB * KB
NBAND = H // QB
STRIPS = NBAND + 1
HP = STRIPS * QB
KA = QB * KB
KBB = NK - KA
PAIRS = HEADS1 // 2
VW = 2 * DH
BAND = QB * W
VSTORES = 2
VLOADS = QB
NEG = -1.0e30
UNITS = NBAND * PAIRS
OHALF, OROW = (0, 0, 1), (0, 64, 0)
ORDER = (0, 2, 1)
DUOS = (UNITS + 1) // 2
STEPS = NBAND * DUOS

SUM0 = 6
SQ0 = SUM0 + 3
VAR0 = SQ0 + 4
CENTRE0 = VAR0 + 2
CHUNK0 = CENTRE0 + 6
PERIOD = 4
END0 = CHUNK0 + PERIOD * (TT - 1) + 10
OUT0 = END0 + 4
STAT1 = OUT0 + 8
SQ1 = (OUT0 + 6, STAT1 + 2)
VAR1 = STAT1 + 5
HEAD1 = max(VAR1 + 3, STEPS)
SLOTS = max(HEAD1 + 4, STEPS + 6)
PIECES = 4
PIECE = NPIX // PIECES


def schedule():
    slots = [[] for _ in range(SLOTS)]
    for b in range(NBAND):
        s = DUOS * b
        if b + 2 < NBAND:
            slots[s + 1].append((0, "qk", b + 2, 0))
            slots[s + 2].append((0, "qk", b + 2, 1))
            slots[s + 4].append((0, "qk", b + 2, 2))
            for n in range(2):
                slots[s + 5 + 2 * n].append((0, "v", b + 2, n))
        for half in range(2):
            slots[s + 15 + half].append((0, "proj", b, half))
    slots[SUM0 + 2].append((1, "mean", 0))
    slots[VAR0].append((1, "var", 0))
    slots[CENTRE0 + 1].append((1, "centres"))
    slots[CENTRE0 + 2].append((1, "norms"))
    slots[CENTRE0 + 6].append((1, "pixels"))
    for n in range(TT):
        c = CHUNK0 + PERIOD * n
        for f in range(4):
            slots[c + 1 + f // 2].append((1, "feat", n, f))
        slots[c + 3] += [(1, "tok", n, 0), (1, "tok", n, 1)]
        slots[c + 9].append((1, "sums", n))
    slots[END0 + 1].append((1, "sumsT"))
    slots[END0 + 2].append((1, "agg"))
    slots[END0 + 3].append((1, "gout"))
    for n in range(16):
        slots[OUT0 + n // 2].append((1, "out0", n))
    slots[OUT0 + 5].append((1, "mean", 1))
    slots[STAT1 + 1].append((1, "mean", 2))
    slots[VAR1].append((1, "var", 1))
    for b in range(2):
        for k in range(3):
            slots[HEAD1 + 2 * b].append((1, "qk", b, k))
        for n in range(2):
            slots[HEAD1 + 2 * b + 1].append((1, "v", b, n))
    return slots


JOBS = schedule()
MEANS = ((0, 2), (0, 1), (1, 2))
BY = {"qk": ("act", "dve", "act"), "v": "dve", "proj": "dve", "mean": "dve", "var": "dve",
      "centres": "dve", "norms": "dve", "pixels": "dve", "feat": "act", "tok": "act",
      "sums": "dve", "sumsT": "dve", "agg": "dve", "gout": "dve", "out0": "dve"}


def emptier(job):
    by = BY[job[1]]
    return by if isinstance(by, str) else by[job[3]]


ORDERED = [job for jobs in JOBS for job in jobs]
BANK = {job: n % 2 for n, job in enumerate(ORDERED)}
NTH = {job: 1 + sum(j[0] == job[0] for j in ORDERED[:n]) for n, job in enumerate(ORDERED)}
NTH_BY = {job: 1 + sum(j[0] == job[0] and emptier(j) == emptier(job) for j in ORDERED[:n])
          for n, job in enumerate(ORDERED)}


def before(job, turns):
    ran = [j for j in ORDERED if j[0] in turns]
    had = [j for j in ran[:ran.index(job)] if BANK[j] == BANK[job]]
    return had[-1] if had else None


def build(nc, x, w1t, w1n, wvt, w2t, b2, alpha, beta, qk, qb, kb, vt, pt, pb, table, ident, gmat, hsum,
          hmask, fsel, cmask, tie, qscale, out, scratch, vmap):
    ctx = ExitStack()
    with ctx:
        def sb(name, shape, dt=F32):
            return ctx.enter_context(nc.sbuf_tensor(name, shape, dt))

        class Signal:

            def __init__(self, name, per, once=0):
                self.sem, self.per, self.once = ctx.enter_context(nc.semaphore(name)), per, once

            def at(self, img, k):
                return img * self.per + (self.once + k)

        KP = (HC + 1, HC)

        xbuf = [sb(f"xbuf{n}", [HC + 1, 2, NPIX]) for n in range(2)]
        xband = sb("xband", [HC + 1, 2, 2, BAND])
        kpad = sb("kpad", [128, 2, WP * WP])
        qbd = sb("qbd", [128, 3, 2, NBAND, 128])
        vring = sb("vring", [KA, 3, NBAND, PAIRS * VW])
        vst = sb("vst", [TOK, 2, BAND // TOK, PAIRS * VW])
        msc = sb("msc", [128, 2, 2, NK])
        nmx = sb("nmx", [128, 2, 2])
        prob = sb("prob", [128, 3, 2, 2 * KA])
        probT = sb("probT", [KA, 3, 512])
        den = sb("den", [128, 2, 2])
        rden = sb("rden", [128, 2, 2])
        ochan = sb("ochan", [128, 2, BAND])
        bmask = sb("bmask", [128, PAIRS, NK])
        wq = sb("wq", [HC + 1, 2, 4, D0 + HM]); w1n_s = sb("w1n_s", [128, 2, C + 1])
        wvt_s = sb("wvt_s", [HC + 1, 2, D0]); w2t_s = sb("w2t_s", [128, 2, C])
        qk_s = sb("qk_s", [HC, 2, 2 * C]); vt_s = sb("vt_s", [HC + 1, 2, C]); pt_s = sb("pt_s", [128, 2, C])
        cols = sb("cols", [128, 24])
        id_s = sb("id_s", [128, 128]); g_s = sb("g_s", [HC, HC]); hsum_s = sb("hsum_s", [128, 128])
        hmask_s = sb("hmask_s", [128, 2, 128])
        fsel_s = sb("fsel_s", [16, 128]); cmask_s = sb("cmask_s", [128, 16]); tie_s = sb("tie_s", [TOK, 4])
        halfs = sb("halfs", [128, 32])
        nhalf = sb("nhalf", [128, 2])
        ones = sb("ones", [128, 1])
        psums = sb("psums", [HC, 2, 16]); ssum = sb("ssum", [HC, 2]); nmean = sb("nmean", [HC, 2])
        ssq = sb("ssq", [HC, 2 * PIECES]); veps = sb("veps", [HC, 2, 2]); osum = sb("osum", [HC, 2, 8])
        rstd = sb("rstd", [HC + 1, 2, 2]); nmr = sb("nmr", [HC + 1, 2, 2]); r196 = sb("r196", [HC, 2])
        junk = sb("junk", [HC, PIECE], mybir.dt.bfloat16)
        pooled = sb("pooled", [HC + 1, 2, 16]); pooledT = sb("pooledT", [16, C + 1])
        cent = sb("cent", [128, 32]); csq = sb("csq", [128, 32]); cn2 = sb("cn2", [128, 32])
        cnrm = sb("cnrm", [128, 32]); rcn = sb("rcn", [128, 32]); cn = sb("cn", [128, 2, 16]); cbd = sb("cbd", [128, 2, 64])
        xtok = sb("xtok", [HC + 1, 2, 2, BAND])
        sq = sb("sq", [TOK, 4, D0])
        nd = sb("nd", [TOK, 2, 32 + 128])
        rn = sb("rn", [TOK, 32]); rm = sb("rm", [TOK, 32]); zz = sb("zz", [TOK, 128]); ee = sb("ee", [TOK, 128])
        mx = sb("mx", [TOK, 32]); sim = sb("sim", [TOK, 128]); key = sb("key", [TOK, 128]); won = sb("won", [TOK, 128])
        xT = sb("xT", [TOK, 2, 4, C + 1])
        yacc = sb("yacc", [128, C + 2])
        rcnt = sb("rcnt", [128, 2]); ys = sb("ys", [128, C + 1]); ysT = sb("ysT", [HC + 1, 2, 128])
        agg = sb("agg", [128, 2, 128]); gout = sb("gout", [128, C]); simT = sb("simT", [128, TT * TOK])
        NA, NBETA = cols[0:TOK, 0:1], cols[0:TOK, 1:2]
        B2 = [cols[0:HC, 2 + t:3 + t] for t in range(2)]
        PB = [cols[0:HC, 4 + t:5 + t] for t in range(2)]
        SCALE = [cols[:, 10 + e:11 + e] for e in range(2)]
        QBIAS, KBIAS = (lambda t: cols[:, 6 + t:7 + t]), (lambda t: cols[:, 8 + t:9 + t])
        SBIAS = [[cols[:, 12 + 2 * t + e:13 + 2 * t + e] for e in range(2)] for t in range(2)]

        bank = [ctx.enter_context(nc.psum_tensor(f"bank{i}", [128, 512], F32)) for i in range(8)]
        psS, psT, psO, psX = bank[0:2], bank[2:4], bank[4:6], bank[6:8]

        def rows(a, w=W):
            return a.rearrange("p (r c) -> p r c", c=w)

        everywhere = lambda a: bass.AP(a.tensor, 0, [[0, TOK], [1, 1]])
        by_fold = lambda lo, hi: bass.AP(w1t.tensor, lo * D0, [[D0, hi - lo], [0, 4], [1, D0]])
        consts = ((wq[0:HC + 1, 0, :, 0:D0], by_fold(0, HC + 1)), (wq[0:HC, 1, :, 0:D0], by_fold(HC + 1, C + 1)),
                  (w1n_s[:, :, :], w1n), (w2t_s[:, :, :], w2t),
                  (wvt_s[0:HC + 1, 0, :], wvt[0:HC + 1]), (wvt_s[0:HC, 1, :], wvt[HC + 1:C + 1]),
                  (vt_s[0:HC + 1, 0, :], vt[0:HC + 1]), (vt_s[0:HC, 1, :], vt[HC + 1:C + 1]),
                  (qk_s[:, :, :], qk), (pt_s[:, 0, :], pt[0:128]), (pt_s[0:64, 1, :], pt[128:C]),
                  (cols[0:TOK, 16:17], everywhere(alpha)), (cols[0:TOK, 17:18], everywhere(beta)),
                  (cols[0:HC, 2:4], b2), (cols[0:HC, 4:6], pb), (cols[:, 6:7], qb[0:128]),
                  (cols[0:64, 7:8], qb[128:C]), (cols[:, 8:9], kb[0:128]), (cols[64:128, 9:10], kb[128:C]),
                  (cols[:, 10:12], qscale), (id_s[:, :], ident), (g_s[:, :], gmat), (hsum_s[:, :], hsum),
                  (hmask_s[:, :, :], hmask), (fsel_s[:, :], fsel), (cmask_s[:, :], cmask),
                  (tie_s[:, :], tie))
        CONSTS = 16 * len(consts)

        s_const = Signal("consts_loaded", 0)
        s_init = Signal("fills_done", 0)
        s_rows = Signal("bias_rows_filled", 0)
        s_fill = Signal("mask_filled", 0)
        s_scat = Signal("bias_scattered", 0)
        s_mask = Signal("mask_loaded", 0)
        s_sbias = Signal("query_bias_scaled", 0)
        s_neg = Signal("alpha_beta_negated", 0)
        s_x, s_xlast = ([Signal(f"{name}_loaded_in_{n}", 8 * m, once=8 * m * (2 - n)) for n in range(2)]
                        for name, m in (("bands", NBAND - 1), ("last_band", 1)))
        s_st = Signal("bands_stored", 16 * NBAND)
        s_zero = Signal("value_tile_zeroed", 0)
        s_frame = Signal("value_frame_stored", 0)
        s_vst = Signal("values_stored", 16 * VSTORES * NBAND)
        s_vload = Signal("value_strips_loaded", 16 * VLOADS * STRIPS)
        s_pool = Signal("pool_sums_ready", 8)
        s_sum = Signal("channel_sums_ready", 3)
        s_nmean = Signal("minus_means_ready", 3)
        s_sq = Signal("square_sums_ready", 4 * PIECES)
        s_vred = Signal("variances_ready", 2)
        s_veps = Signal("variance_eps_ready", 2)
        s_rstd = Signal("rstd_ready", 2)
        s_nmr = Signal("shift_ready", 3)
        s_pooled = Signal("pooled_ready", 1)
        s_cent = Signal("centres_copied", 1)
        s_csq = Signal("centre_squares_ready", 1)
        s_cn2 = Signal("centre_norms2_copied", 1)
        s_crt = Signal("centre_norms_ready", 2)
        s_cchain = Signal("centre_steps", 6)
        s_cbd = Signal("centres_spread", 1)
        s_xtok = Signal("chunk_normalised", TT)
        s_nd = Signal("token_norms2_ready", 2 * TT)
        s_nrt = Signal("token_norms_ready", 2 * TT)
        s_rn = Signal("token_norm_steps", 2 * TT)
        s_z = Signal("cosines_ready", TT)
        s_e = Signal("sigmoid_exp_ready", TT)
        s_chain = Signal("argmax_steps", 7 * TT)
        s_won = Signal("similarities_masked", TT)
        s_rc = Signal("count_steps", 2)
        s_ys = Signal("cluster_sums_scaled", 1)
        s_xband = Signal("band_normalised", NBAND)
        s_begun = {e: Signal(f"step_begun_by_{e}", 0) for e in ("dve", "pool", "sp")}
        s_scores = Signal("scores_ready", STEPS)
        s_max = Signal("maxima_ready", STEPS)
        s_exp = Signal("probabilities_ready", STEPS)
        s_tr = Signal("probabilities_transposed", STEPS)
        s_trs = Signal("probabilities_transposed_copied", STEPS)
        s_av = Signal("attention_ready", NBAND * PAIRS)
        s_rden = Signal("row_sums_inverted", STEPS)
        s_norm = Signal("probabilities_divided", STEPS)
        s_on = Signal("attention_copied", NBAND * PAIRS)
        count = lambda turn, e=None: sum(j[0] == turn and e in (None, emptier(j)) for j in ORDERED)
        s_job = [Signal(f"side_jobs{t}_filled", count(t)) for t in range(2)]
        s_emp = {(t, e): Signal(f"side_jobs{t}_emptied_by_{e}", count(t, e), once=1) for t in range(2) for e in ("act", "dve")}

        finished = {}
        for g in range(NBAND * PAIRS):
            last_unit = NBAND * (g % PAIRS) + NBAND - 1
            finished.setdefault(DUOS * (g // PAIRS) + last_unit // 2, []).append(g)

        through = {}
        for d, groups in finished.items():
            through.setdefault(d + 4 - d % 2, []).extend(groups)

        def units(d):
            b, j = divmod(d, DUOS)
            return [(b, u % NBAND, ORDER[u // NBAND]) for u in range(2 * j, min(2 * j + 2, UNITS))]

        def chunk(slot, phase):
            n, r = divmod(slot - CHUNK0 - phase, PERIOD)
            return n if r == 0 and 0 <= n < TT else None

        def images(engine, turn, then=lambda: None):
            turn(0, 1, (1,))
            then()
            with engine.Fori(0, B // 2 - 1) as two:
                turn(two * 2, 0, (0, 1))
                turn(two * 2 + 1, 1, (0, 1))
            turn(B - 2, 0, (0, 1))
            turn(B - 1, 1, (0,))

        block = ctx.enter_context(nc.Block())

        @block.sync
        def _(sp):
            def load(img, n, b):
                sp.dma_start(xbuf[n][0:HC, :, b * BAND:(b + 1) * BAND],
                             x[bass.ds(img, 1), :, b * BAND:(b + 1) * BAND].rearrange("o (t p) n -> p (o t) n", p=HC))\
                    .then_inc((s_x if b < NBAND - 1 else s_xlast)[n].sem, 16)

            for b in range(NBAND):
                load(0, 0, b)
            for dst, src in consts:
                sp.dma_start(dst, src).then_inc(s_const.sem, 16)
            sp.wait_ge(s_zero.sem, 1)
            vrow = WP * PAIRS * VW
            for r in range(0, HP, 8):
                dst = bass.AP(vmap.tensor, r * vrow, [[PAIRS * VW, WP], [vrow, 8], [1, PAIRS * VW]])
                sp.dma_start(dst, vst[0:WP, :, :, :].rearrange("p a n v -> p (a n) v")).then_inc(s_frame.sem, 16)
            for b in range(NBAND):
                load(1, 1, b)
            sp.wait_ge(s_fill.sem, 1)
            row = PAIRS * NK
            sp.dma_start(scratch.rearrange("(p n) -> p n", n=row), bmask[:, :, :].rearrange("p a n -> p (a n)"))\
                .then_inc(s_scat.sem, 16)
            sp.wait_ge(s_scat.sem, 16)
            for par in range(2):
                for pair in range(PAIRS):
                    for r in range(QB):
                        first = (par * 64 + r * QB) * row + pair * NK + r * KB
                        dst = bass.AP(scratch.tensor, first, [[row + 1, QB], [KB, WIN], [1, WIN]])
                        src = bass.AP(table.tensor, (2 * pair + par) * WIN * WIN, [[0, QB], [WIN, WIN], [1, WIN]])
                        sp.dma_start(dst, src).then_inc(s_scat.sem, 16)
            sp.wait_ge(s_scat.sem, 16 * (1 + 2 * PAIRS * QB))
            sp.dma_start(bmask[:, :, :].rearrange("p a n -> p (a n)"), scratch.rearrange("(p n) -> p n", n=row))\
                .then_inc(s_mask.sem, 16)
            sp.wait_ge(s_frame.sem, 16 * HP // 8)

            def took_wait():
                sp.sem_inc(s_begun["sp"].sem, 1)

            def last_strip_loaded(img, s):
                if s or not (isinstance(img, int) and img == 0):
                    sp.wait_ge(s_vload.sem, s_vload.at(img, 16 * VLOADS * s))

            def store_values(img, turn, b):
                sp.wait_ge(s_emp[turn, "dve"].sem, s_emp[turn, "dve"].at(img, NTH_BY[turn, "v", b, 1]))
                took_wait()
                last_strip_loaded(img, b if b >= 2 else 0)
                for r in range(VSTORES):
                    dst = bass.AP(vmap.tensor, (PAD + QB * b + r) * vrow + PAD * PAIRS * VW,
                                  [[PAIRS * VW, W], [VSTORES * vrow, BAND // TOK], [1, PAIRS * VW]])
                    sp.dma_start(dst, vst[W * r:W * r + W, b % 2, :, :]).then_inc(s_vst.sem, 16)

            def load_strip(img, s, turns):
                sp.wait_ge(s_vst.sem, s_vst.at(img, 16 * VSTORES * min(max(s + 1, 2), NBAND)))
                if s >= 3 or s < 2 and 0 in turns:
                    took_wait()
                if s >= 3:
                    sp.wait_ge(s_av.sem, s_av.at(img, PAIRS * (s - 2)))
                elif 0 in turns and s < 2:
                    sp.wait_ge(s_av.sem, s_av.at(img, 0))
                if s >= NBAND:
                    took_wait()
                    last_strip_loaded(img, s)
                for r in range(VLOADS):
                    n = KA // VLOADS
                    src = bass.AP(vmap.tensor, (QB * s + r) * vrow, [[PAIRS * VW, n], [QB * PAIRS * VW, NBAND], [1, PAIRS * VW]])
                    sp.dma_start(vring[n * r:n * r + n, s % 3, :, :], src).then_inc(s_vload.sem, 16)

            def renew(img, n, b, more):
                if more:
                    sp.wait_ge(s_st.sem, s_st.at(img, 16 * (b + 1)))
                    load(img + 2, n, b)

            def turn(img, n, turns, more=False):
                nxt = img + 1 if 0 in turns else img
                for slot in range(SLOTS):
                    b, j = divmod(slot, DUOS)
                    if 0 in turns and j == 4 and 2 <= b < NBAND:
                        renew(img, n, b - 2, more)
                    if 0 in turns and j == 8 and b + 2 < STRIPS:
                        if b + 2 < NBAND:
                            store_values(img, 0, b + 2)
                        load_strip(img, b + 2, turns)
                    if 0 in turns and slot == SLOTS - 4:
                        renew(img, n, NBAND - 2, more)
                    if 0 in turns and j == 9 and b >= 1:
                        store(img, n, b - 1)
                    for b in range(2):
                        if 1 in turns and slot == HEAD1 + 2 * b + 1:
                            store_values(nxt, 1, b)
                    if 1 in turns and slot == HEAD1 + 3:
                        for b in range(2):
                            load_strip(nxt, b, turns)
                if 0 in turns:
                    store(img, n, NBAND - 1)
                    renew(img, n, NBAND - 1, more)

            def store(img, n, b):
                sp.wait_ge(s_emp[0, "dve"].sem, s_emp[0, "dve"].at(img, NTH_BY[0, "proj", b, 1]))
                sp.dma_start(out[bass.ds(img, 1), :, b * BAND:(b + 1) * BAND].rearrange("o (t p) n -> p (o t) n", p=HC),
                             xbuf[n][0:HC, :, b * BAND:(b + 1) * BAND]).then_inc(s_st.sem, 16)

            turn(0, 1, (1,))
            with sp.Fori(0, B // 2 - 1) as two:
                for n in range(2):
                    turn(two * 2 + n, n, (0, 1), more=True)
            turn(B - 2, 0, (0, 1))
            turn(B - 1, 1, (0,))
            sp.wait_ge(s_st.sem, 16 * NBAND * B)

        @block.gpsimd
        def _(pool):
            nc.gpsimd.memset(kpad[:, :, :], 0.0).then_inc(s_init.sem, 1)
            nc.gpsimd.memset(prob[:, :, :, :], 0.0).then_inc(s_init.sem, 1)
            nc.gpsimd.memset(halfs[:, :], 0.5).then_inc(s_init.sem, 1)
            nc.gpsimd.memset(nhalf[:, :], -0.5).then_inc(s_init.sem, 1)
            nc.gpsimd.memset(ones[:, :], 1.0).then_inc(s_init.sem, 1)
            nc.gpsimd.memset(bmask[:, :, :], NEG).then_inc(s_fill.sem, 1)

            def turn(img, n, turns):
                nxt = img + 1 if 0 in turns else img
                xn = xbuf[1 - n]
                for slot in range(SLOTS):
                    if 1 not in turns:
                        continue
                    for g, at in ((0, VAR0 + 1), (1, VAR1 + 1)):
                        if slot == at:
                            pool.wait_ge(s_veps.sem, s_veps.at(nxt, g + 1))
                            nc.gpsimd.tensor_tensor(rstd[0:HC, g, :], veps[:, g, :], nhalf[0:HC, :], ALU.pow)\
                                .then_inc(s_rstd.sem, 1)
                    if slot == CENTRE0 + 3:
                        pool.wait_ge(s_cn2.sem, s_cn2.at(nxt, 1))
                        for m in range(2):
                            q = slice(16 * m, 16 * m + 16)
                            nc.gpsimd.tensor_tensor(cnrm[:, q], cn2[:, q], halfs[:, q], ALU.pow).then_inc(s_crt.sem, 1)
                    if (c := chunk(slot, -1)) is not None:
                        pool.wait_ge(s_nmr.sem, s_nmr.at(nxt, 2))
                        pool.sem_inc(s_begun["pool"].sem, 1)
                        for t in range(2):
                            for fh in range(2):
                                src = rows(xn[:, t, :])[:, FOLD * fh + TR * c:FOLD * fh + TR * c + TR, :]
                                dst = xtok[:, c % 2, t, 2 * TOK * fh:2 * TOK * fh + 2 * TOK]
                                last = nc.gpsimd.tensor_scalar(dst.rearrange("p (f r c) -> p f r c", f=2, r=TR),
                                                               src.rearrange("p r (f c) -> p f r c", f=2),
                                                               rstd[:, 0, t:t + 1], nmr[:, 0, t:t + 1], ALU.mult, ALU.add)
                        last.then_inc(s_xtok.sem, 1)
                    for h in range(2):
                        if (c := chunk(slot, 2 + h)) is not None:
                            q = slice(16 * h, 16 * h + 16)
                            pool.wait_ge(s_nd.sem, s_nd.at(nxt, 2 * c + h + 1))
                            nc.gpsimd.tensor_tensor(rn[:, q], nd[:, c % 2, q], halfs[0:TOK, q], ALU.pow).then_inc(s_nrt.sem, 1)

            images(pool, turn)

        @block.scalar
        def _(act):
            act.wait_ge(s_const.sem, CONSTS)
            act.wait_ge(s_init.sem, 5)
            for t in range(2):
                act.sem_inc(s_emp[t, "act"].sem, 1)
            for t, p in ((0, 128), (1, 64)):
                for e in range(2):
                    nc.scalar.activation(SBIAS[t][e][0:p], QBIAS(t)[0:p], ACT.Identity, bias=0.0,
                                         scale=SCALE[e][0:p]).then_inc(s_sbias.sem, 1)
            act.wait_ge(s_sbias.sem, 4)
            act.wait_ge(s_neg.sem, 1)

            def squares(nxt, xn, g, first, last):
                if first == 0 or (g, first) == (1, PIECES):
                    act.wait_ge(s_nmean.sem, s_nmean.at(nxt, 1 + (g and 1 + first // PIECES)))
                for piece in range(first, last):
                    t, k = divmod(piece, PIECES)
                    done = 2 * PIECES * g + piece
                    if done:
                        act.wait_ge(s_sq.sem, s_sq.at(nxt, done))
                    nc.scalar.activation(junk[:, :], xn[0:HC, t, PIECE * k:PIECE * k + PIECE], ACT.Square,
                                         bias=nmean[:, t:t + 1], scale=1.0, accum_out=ssq[:, PIECES * t + k:PIECES * t + k + 1])\
                        .then_inc(s_sq.sem, 1)

            def empty(img, job):
                turn, kind, b = job[0:3]
                act.wait_ge(s_job[turn].sem, s_job[turn].at(img, NTH[job]))
                ps = psX[BANK[job]]
                if kind == "qk":
                    half, p = (0, 128) if job[3] == 0 else (1, 64)
                    for e in range(2):
                        dst = qbd[0:p, b % 3, half, :, 64 * e:64 * e + 64].rearrange("p n (r c) -> p n r c", c=QB)
                        last = nc.scalar.activation(dst, ps[0:p, 0:BAND].rearrange("p (r n c) -> p n r c", n=NBAND, c=QB),
                                                    ACT.Identity, bias=SBIAS[half][e][0:p], scale=SCALE[e][0:p])
                    if half:
                        dst = rows(kpad[0:64, 1, :], WP)[:, PAD + QB * b:PAD + QB * b + QB, PAD:PAD + W]
                        last = nc.scalar.activation(dst, rows(ps[64:128, 0:BAND]), ACT.Identity, bias=KBIAS(1)[64:128], scale=1.0)
                elif kind == "feat":
                    f = job[3]
                    if f == 0 and b > 0:
                        act.wait_ge(s_nd.sem, s_nd.at(img, 2 * b))
                    if f == 0 and b > 1:
                        act.wait_ge(s_z.sem, s_z.at(img, b - 1))
                    nc.scalar.activation(sq[:, f, :], ps[0:TOK, 0:D0], ACT.Square)
                    last = nc.scalar.activation(nd[:, b % 2, 32 + HM * f:32 + HM * f + HM], ps[0:TOK, D0:D0 + HM], ACT.Copy)
                elif kind == "tok":
                    last = nc.scalar.activation(xT[:, b % 2, 2 * job[3]:2 * job[3] + 2, :].rearrange("p a n -> p (a n)"),
                                                ps[0:TOK, 0:2 * (C + 1)], ACT.Copy)
                last.then_inc(s_emp[turn, "act"].sem, 1)

            def turn(img, n, turns):
                nxt = img + 1 if 0 in turns else img
                xn = xbuf[1 - n]
                for slot in range(SLOTS):
                    if 0 in turns and slot < STEPS:
                        act.wait_ge(s_max.sem, s_max.at(img, slot + 1))
                        if slot >= 3:
                            act.wait_ge(s_tr.sem, s_tr.at(img, slot - 2))
                        for j in range(len(units(slot))):
                            last = nc.scalar.activation(prob[:, slot % 3, j, 0:NK], msc[:, slot % 2, j, :], ACT.Exp,
                                                        bias=nmx[:, slot % 2, j:j + 1], scale=-1.0,
                                                        accum_out=den[:, slot % 2, j:j + 1])
                        last.then_inc(s_exp.sem, 1)
                    d = slot - 2
                    if 0 in turns and 0 <= d < STEPS:
                        m = 256 * len(units(d))
                        act.wait_ge(s_tr.sem, s_tr.at(img, d + 1))
                        nc.scalar.activation(probT[:, d % 3, 0:m], psT[d % 2][0:KA, 0:m], ACT.Copy).then_inc(s_trs.sem, 1)
                    for g in through.get(slot, []) if 0 in turns else ():
                        act.wait_ge(s_av.sem, s_av.at(img, g + 1))
                        pair = ORDER[g % PAIRS]
                        q = slice(OROW[pair], OROW[pair] + VW)
                        dst = ochan[q, OHALF[pair], :].rearrange("p (r n c) -> p n r c", n=NBAND, c=QB)
                        nc.scalar.activation(dst, psO[g % 2][q, 0:BAND].rearrange("p (n r c) -> p n r c", n=NBAND, c=QB),
                                             ACT.Copy).then_inc(s_on.sem, 1)
                    for job in JOBS[slot]:
                        if job[0] in turns and emptier(job) == "act":
                            empty(nxt if job[0] else img, job)
                    if 1 not in turns:
                        continue
                    for g, at, first, m in ((0, SQ0, 0, 4), (1, SQ1[0], 0, 2), (1, SQ1[1], PIECES, 2)):
                        if 0 <= slot - at < m:
                            squares(nxt, xn, g, first + 2 * (slot - at), first + 2 * (slot - at) + 2)
                    if (c := chunk(slot, 6)) is not None:
                        act.wait_ge(s_z.sem, s_z.at(nxt, c + 1))
                        nc.scalar.activation(ee[:, :], zz[:, :], ACT.Exp, bias=NBETA, scale=NA).then_inc(s_e.sem, 1)

            images(act, turn)

        @block.vector
        def _(dve):
            dve.wait_ge(s_const.sem, CONSTS)
            dve.wait_ge(s_init.sem, 5)
            for t in range(2):
                dve.sem_inc(s_emp[t, "dve"].sem, 1)
            nc.vector.memset(vst[:, :, :, :], 0.0).then_inc(s_zero.sem, 1)
            for a, v in ((xbuf[0][HC:HC + 1, :, :], 1.0), (xbuf[1][HC:HC + 1, :, :], 1.0), (pooled[HC:HC + 1, 0, :], 1.0),
                         (rstd[HC:HC + 1, :, :], 1.0), (nmr[HC:HC + 1, :, :], 0.0)):
                nc.vector.memset(a, v).then_inc(s_rows.sem, 1)
            nc.vector.tensor_scalar(cols[0:TOK, 0:2], cols[0:TOK, 16:18], -1.0, None, ALU.mult).then_inc(s_neg.sem, 1)
            dve.wait_ge(s_rows.sem, 5)

            def shift(nxt, g):
                dve.wait_ge(s_rstd.sem, s_rstd.at(nxt, g + 1))
                nc.vector.tensor_tensor(nmr[0:HC, g, :], nmean[:, :], rstd[0:HC, g, :], ALU.mult).then_inc(s_nmr.sem, 1)

            def normal_band(img, xb, b):
                for t in range(2):
                    last = nc.vector.tensor_scalar(xband[:, b % 2, t, :], xb[:, t, BAND * b:BAND * b + BAND],
                                                   rstd[:, 1, t:t + 1], nmr[:, 1, t:t + 1], ALU.mult, ALU.add)
                last.then_inc(s_xband.sem, 1)

            def empty(img, xb, xn, job, turns):
                turn, kind = job[0:2]
                dve.wait_ge(s_job[turn].sem, s_job[turn].at(img, NTH[job]))
                ps = psX[BANK[job]]
                if kind == "qk":
                    b = job[2]
                    dst = rows(kpad[:, 0, :], WP)[:, PAD + QB * b:PAD + QB * b + QB, PAD:PAD + W]
                    last = nc.vector.tensor_scalar(dst, rows(ps[:, 0:BAND]), KBIAS(0), None, ALU.add)
                elif kind == "v":
                    b, k0 = job[2], 2 * job[3]
                    if turns == (1,) and b == 0 and k0 == 0:
                        dve.wait_ge(s_frame.sem, 16 * HP // 8)
                    last = nc.vector.tensor_copy(vst[:, b % 2, k0:k0 + 2, :].rearrange("p n v -> p (n v)"), ps[0:TOK, 0:2 * C])
                elif kind == "proj":
                    b, t = job[2:]
                    pix = xb[0:HC, t, b * BAND:(b + 1) * BAND]
                    last = nc.vector.scalar_tensor_tensor(pix, ps[0:HC, 0:BAND], PB[t], pix, ALU.add, ALU.add)
                elif kind == "mean":
                    t0, t1 = MEANS[job[2]]
                    last = nc.vector.tensor_scalar(nmean[:, t0:t1], ps[0:HC, 0:t1 - t0], -1.0, None, ALU.mult)
                    last.then_inc(s_nmean.sem, 1)
                    last = nc.vector.memset(rcnt[0:1, 1:2], 0.0)
                elif kind == "var":
                    g = job[2]
                    nc.vector.tensor_reduce(veps[:, g, :], ps[0:HC, 0:2 * PIECES].rearrange("p (t k) -> p t k", t=2),
                                            AX.X, ALU.add).then_inc(s_vred.sem, 1)
                    dve.wait_ge(s_vred.sem, s_vred.at(img, g + 1))
                    nc.vector.tensor_scalar(veps[:, g, :], veps[:, g, :], EPS, None, ALU.add).then_inc(s_veps.sem, 1)
                    last = nc.vector.memset(rcnt[0:1, 1:2], 0.0)
                elif kind == "centres":
                    nc.vector.tensor_copy(cent[:, :], ps[:, 0:32]).then_inc(s_cent.sem, 1)
                    last = nc.vector.tensor_copy(pooledT[:, :], ps[0:16, 64:64 + C + 1])
                elif kind == "norms":
                    nc.vector.tensor_copy(cn2[:, :], ps[:, 0:32]).then_inc(s_cn2.sem, 1)
                    last = nc.vector.memset(rcnt[0:1, 1:2], 0.0)
                elif kind == "pixels":
                    for t in range(2):
                        src = ps[0:KP[t], 128 * t:128 * t + 128].rearrange("p (m f n) -> p m f n", m=2, f=4)
                        last = nc.vector.tensor_copy(wq[0:KP[t], t, :, D0:D0 + HM].rearrange("p f (m n) -> p m f n", m=2), src)
                elif kind == "sums":
                    c = job[2]
                    if c == 0:
                        nc.vector.tensor_copy(yacc[:, :], ps[:, 0:C + 2])
                    else:
                        nc.vector.tensor_tensor(yacc[:, :], ps[:, 0:C + 2], yacc[:, :], ALU.add)
                    last = nc.vector.tensor_copy(simT[:, TOK * c:TOK * c + TOK], ps[:, 256:256 + TOK])
                elif kind == "sumsT":
                    nc.vector.tensor_copy(ysT[0:HC + 1, 0, :], ps[0:HC + 1, 0:128])
                    last = nc.vector.tensor_copy(ysT[0:HC, 1, :], ps[0:HC, 128:256])
                elif kind == "agg":
                    last = nc.vector.tensor_tensor(agg[:, :, :].rearrange("p m n -> p (m n)"), ps[:, 0:256],
                                                   hmask_s[:, :, :].rearrange("p m n -> p (m n)"), ALU.mult)
                elif kind == "gout":
                    last = nc.vector.tensor_copy(gout[:, :], ps[:, 0:C])
                elif kind == "out0":
                    t, hf, f = job[2] // 8, job[2] // 4 % 2, job[2] % 4
                    nr = 16 if hf == 0 else 12
                    r0, c0 = FOLD * (f // 2) + 16 * hf, FOLD * (f % 2)
                    pix = rows(xn[0:HC, t, :])[:, r0:r0 + nr, c0:c0 + FOLD]
                    last = nc.vector.scalar_tensor_tensor(pix, rows(ps[0:HC, 0:nr * FOLD], FOLD), B2[t], pix, ALU.add, ALU.add,
                                                          accum_out=osum[:, t, job[2] % 8:job[2] % 8 + 1])
                last.then_inc(s_emp[turn, "dve"].sem, 1)

            def turn(img, n, turns):
                nxt = img + 1 if 0 in turns else img
                xb, xn = xbuf[n], xbuf[1 - n]
                for slot in range(SLOTS):
                    b, j = divmod(slot, DUOS)
                    if 0 in turns and slot < STEPS:
                        dve.wait_ge(s_scores.sem, s_scores.at(img, slot + 1))
                        dve.sem_inc(s_begun["dve"].sem, 1)
                        for k, (_, _, pair) in enumerate(units(slot)):
                            last = nc.vector.tensor_tensor_reduce(
                                out=msc[:, slot % 2, k, :], in0=psS[slot % 2][:, k * NK:(k + 1) * NK], in1=bmask[:, pair, :],
                                scale=-1.0, scalar=3.0e38, op0=ALU.add, op1=ALU.min, accum_out=nmx[:, slot % 2, k:k + 1])
                        last.then_inc(s_max.sem, 1)
                    d = slot - 1
                    if 0 in turns and 0 <= d < STEPS:
                        m = len(units(d))
                        dve.wait_ge(s_exp.sem, s_exp.at(img, d + 1))
                        nc.vector.reciprocal(rden[:, d % 2, 0:m], den[:, d % 2, 0:m]).then_inc(s_rden.sem, 1)
                        dve.wait_ge(s_rden.sem, s_rden.at(img, d + 1))
                        for k in range(m):
                            row = prob[:, d % 3, k, 0:NK]
                            last = nc.vector.tensor_scalar(row, row, rden[:, d % 2, k:k + 1], None, ALU.mult)
                        last.then_inc(s_norm.sem, 1)
                    if 0 in turns and j == DUOS - 1 and b + 3 < NBAND:
                        normal_band(img, xb, b + 3)
                    for job in JOBS[slot]:
                        if job[0] in turns and emptier(job) == "dve":
                            empty(nxt if job[0] else img, xb, xn, job, turns)
                    if 1 not in turns:
                        continue
                    for a, t in {SUM0: ((3, 0), (3, 1))}.get(slot, (divmod(slot, 2),) if slot < SUM0 else ()):
                        if slot in (0, SUM0) and t == 0:
                            wait = (s_xlast if slot else s_x)[1 - n]
                            dve.wait_ge(wait.sem, wait.at(nxt, 0))
                        v = xn[0:HC, t, a * POOL * W:(a + 1) * POOL * W].rearrange("p (r b c) -> p b r c", b=4, c=POOL)
                        nc.vector.tensor_reduce(psums[:, t, 4 * a:4 * a + 4], v, AX.XY, ALU.add).then_inc(s_pool.sem, 1)
                    if slot == SUM0:
                        dve.wait_ge(s_pool.sem, s_pool.at(nxt, 8))
                        nc.vector.tensor_reduce(ssum[:, :], psums[:, :, :], AX.X, ALU.add).then_inc(s_sum.sem, 1)
                    if slot == CENTRE0:
                        shift(nxt, 0)
                        nc.vector.tensor_scalar(r196[:, :], rstd[0:HC, 0, :], 1.0 / (POOL * POOL), None, ALU.mult)\
                            .then_inc(s_nmr.sem, 1)
                        dve.wait_ge(s_nmr.sem, s_nmr.at(nxt, 2))
                        for t in range(2):
                            last = nc.vector.tensor_scalar(pooled[0:HC, t, :], psums[:, t, :], r196[:, t:t + 1],
                                                           nmr[0:HC, 0, t:t + 1], ALU.mult, ALU.add)
                        last.then_inc(s_pooled.sem, 1)
                    if slot == CENTRE0 + 1:
                        dve.wait_ge(s_cent.sem, s_cent.at(nxt, 1))
                        nc.vector.tensor_tensor(csq[:, :], cent[:, :], cent[:, :], ALU.mult).then_inc(s_csq.sem, 1)
                    for m in range(2):
                        if slot != CENTRE0 + 4 + m:
                            continue
                        q = slice(16 * m, 16 * m + 16)
                        dve.wait_ge(s_crt.sem, s_crt.at(nxt, m + 1))
                        nc.vector.tensor_scalar(rcn[:, q], cnrm[:, q], 1e-12, None, ALU.max).then_inc(s_cchain.sem, 1)
                        dve.wait_ge(s_cchain.sem, s_cchain.at(nxt, 3 * m + 1))
                        nc.vector.reciprocal(csq[:, q], rcn[:, q]).then_inc(s_cchain.sem, 1)
                        dve.wait_ge(s_cchain.sem, s_cchain.at(nxt, 3 * m + 2))
                        nc.vector.tensor_tensor(cn[:, m, :], cent[:, q], csq[:, q], ALU.mult).then_inc(s_cchain.sem, 1)
                        dve.wait_ge(s_cchain.sem, s_cchain.at(nxt, 3 * m + 3))
                        for f in range(4):
                            src = cn[:, m, :].rearrange("p (a u b v) -> p a b u v", a=2, u=2, b=2)[:, f // 2, f % 2]
                            src = src[:, None, :, :].broadcast_to([128, 4, 2, 2])
                            last = nc.vector.tensor_tensor(cbd[:, m, 16 * f:16 * f + 16].rearrange("p (h u v) -> p h u v", h=4, u=2),
                                                           src, cmask_s[:, :].rearrange("p (h u v) -> p h u v", h=4, u=2), ALU.mult)
                        if m == 1:
                            last.then_inc(s_cbd.sem, 1)
                    by4 = lambda a: a[:, :].rearrange("p (n m) -> p n m", m=4)
                    for h in range(2):
                        if (c := chunk(slot, 2 + h)) is not None:
                            dve.wait_ge(s_emp[1, "act"].sem, s_emp[1, "act"].at(nxt, NTH_BY[1, "feat", c, 2 * h + 1]))
                            nc.vector.tensor_reduce(nd[:, c % 2, 16 * h:16 * h + 16],
                                                    sq[:, 2 * h:2 * h + 2, :].rearrange("p f (h c) -> p (f h) c", c=D0 // HEADS0),
                                                    AX.X, ALU.add).then_inc(s_nd.sem, 1)
                    if (c := chunk(slot, 5)) is not None:
                        dve.wait_ge(s_nrt.sem, s_nrt.at(nxt, 2 * c + 2))
                        nc.vector.tensor_scalar(rm[:, :], rn[:, :], 1e-12, None, ALU.max).then_inc(s_rn.sem, 1)
                        dve.wait_ge(s_rn.sem, s_rn.at(nxt, 2 * c + 1))
                        nc.vector.reciprocal(mx[:, :], rm[:, :]).then_inc(s_rn.sem, 1)
                        dve.wait_ge(s_rn.sem, s_rn.at(nxt, 2 * c + 2))
                        nc.vector.tensor_tensor(by4(zz), nd[:, c % 2, 32:160].rearrange("p (n m) -> p n m", m=4),
                                                mx[:, :, None].broadcast_to([TOK, 32, 4]), ALU.mult).then_inc(s_z.sem, 1)
                    if (c := chunk(slot, 7)) is not None:
                        k = 7 * c
                        top = mx[:, :, None].broadcast_to([TOK, 32, 4])
                        dve.wait_ge(s_e.sem, s_e.at(nxt, c + 1))
                        nc.vector.tensor_scalar(key[:, :], ee[:, :], 1.0, None, ALU.add).then_inc(s_chain.sem, 1)
                        dve.wait_ge(s_chain.sem, s_chain.at(nxt, k + 1))
                        nc.vector.reciprocal(sim[:, :], key[:, :]).then_inc(s_chain.sem, 1)
                        dve.wait_ge(s_chain.sem, s_chain.at(nxt, k + 2))
                        nc.vector.tensor_reduce(mx[:, :], by4(sim), AX.X, ALU.max).then_inc(s_chain.sem, 1)
                        dve.wait_ge(s_chain.sem, s_chain.at(nxt, k + 3))
                        nc.vector.tensor_tensor(by4(key), by4(sim), top, ALU.is_equal).then_inc(s_chain.sem, 1)
                        dve.wait_ge(s_chain.sem, s_chain.at(nxt, k + 4))
                        nc.vector.tensor_tensor(by4(won), by4(key), tie_s[:, None, :].broadcast_to([TOK, 32, 4]), ALU.mult)\
                            .then_inc(s_chain.sem, 1)
                        dve.wait_ge(s_chain.sem, s_chain.at(nxt, k + 5))
                        nc.vector.tensor_reduce(mx[:, :], by4(won), AX.X, ALU.max).then_inc(s_chain.sem, 1)
                        dve.wait_ge(s_chain.sem, s_chain.at(nxt, k + 6))
                        nc.vector.tensor_tensor(by4(key), by4(won), top, ALU.is_equal).then_inc(s_chain.sem, 1)
                        dve.wait_ge(s_chain.sem, s_chain.at(nxt, k + 7))
                        nc.vector.tensor_tensor(won[:, :], sim[:, :], key[:, :], ALU.mult).then_inc(s_won.sem, 1)
                    if slot == END0:
                        dve.wait_ge(s_emp[1, "dve"].sem, s_emp[1, "dve"].at(nxt, NTH_BY[1, "sums", TT - 1]))
                        nc.vector.tensor_scalar(rcnt[:, 0:1], yacc[:, C + 1:C + 2], 1.0, None, ALU.add).then_inc(s_rc.sem, 1)
                        dve.wait_ge(s_rc.sem, s_rc.at(nxt, 1))
                        nc.vector.reciprocal(rcnt[:, 0:1], rcnt[:, 0:1]).then_inc(s_rc.sem, 1)
                        dve.wait_ge(s_rc.sem, s_rc.at(nxt, 2))
                        nc.vector.tensor_scalar(ys[:, :], yacc[:, 0:C + 1], rcnt[:, 0:1], None, ALU.mult).then_inc(s_ys.sem, 1)
                    for t, at in ((0, OUT0 + 4), (1, STAT1)):
                        if slot == at:
                            done = NTH_BY[1, "out0", 8 * t + 7]
                            dve.wait_ge(s_emp[1, "dve"].sem, s_emp[1, "dve"].at(nxt, done))
                            nc.vector.tensor_reduce(ssum[:, t:t + 1], osum[:, t, :], AX.X, ALU.add).then_inc(s_sum.sem, 1)
                    if slot == VAR1 + 2:
                        shift(nxt, 1)
                        dve.wait_ge(s_nmr.sem, s_nmr.at(nxt, 3))
                        normal_band(nxt, xn, 0)
                    if slot == VAR1 + 3:
                        normal_band(nxt, xn, 1)
                    if slot == SLOTS - 1:
                        normal_band(nxt, xn, 2)

            images(dve, turn, lambda: dve.wait_ge(s_mask.sem, 16))

        @block.tensor
        def _(pe):
            mm, mm_t = nc.tensor.matmul, nc.tensor.transpose
            pe.wait_ge(s_const.sem, CONSTS)
            pe.wait_ge(s_init.sem, 5)
            pe.wait_ge(s_rows.sem, 5)

            def wait_emptied(img, nxt, job):
                s = s_emp[job[0], emptier(job)]
                pe.wait_ge(s.sem, s.at(nxt if job[0] else img, NTH_BY[job]))

            def fill(img, nxt, job, turns):
                turn, kind = job[0:2]
                own = nxt if turn else img
                had = before(job, turns)
                if had:
                    wait_emptied(img, nxt, had)
                elif 0 in turns:
                    for e in ("act", "dve"):
                        pe.wait_ge(s_emp[0, e].sem, s_emp[0, e].at(img, 0))
                        pe.wait_ge(s_emp[1, e].sem, s_emp[1, e].at(img, count(1, e)))
                ps = psX[BANK[job]]
                if kind == "qk":
                    b, k = job[2:]
                    pe.wait_ge(s_xband.sem, s_xband.at(own, b + 1))
                    for t in range(2):
                        last = mm(ps[:, 0:BAND], qk_s[:, t, 128 * k:128 * k + 128], xband[0:HC, b % 2, t, :], start=(t == 0), stop=(t == 1))
                elif kind == "v":
                    b = job[2]
                    pe.wait_ge(s_xband.sem, s_xband.at(own, b + 1))
                    for k in range(2):
                        o, q = C * k, TOK * (2 * job[3] + k)
                        for t in range(2):
                            last = mm(ps[0:TOK, o:o + C], xband[0:KP[t], b % 2, t, q:q + TOK], vt_s[0:KP[t], t, :],
                                      start=(t == 0), stop=(t == 1))
                elif kind == "proj":
                    b, t = job[2:]
                    pe.wait_ge(s_on.sem, s_on.at(own, PAIRS * (b + 1)))
                    for e, p in enumerate((128, 64)):
                        last = mm(ps[0:HC, 0:BAND], pt_s[0:p, e, HC * t:HC * t + HC], ochan[0:p, e, :], start=(e == 0), stop=(e == 1))
                elif kind == "mean":
                    pe.wait_ge(s_sum.sem, s_sum.at(own, job[2] + 1))
                    t0, t1 = MEANS[job[2]]
                    last = mm(ps[0:HC, 0:t1 - t0], g_s[:, :], ssum[:, t0:t1], start=True, stop=True)
                elif kind == "var":
                    pe.wait_ge(s_sq.sem, s_sq.at(own, 2 * PIECES * (job[2] + 1)))
                    last = mm(ps[0:HC, 0:2 * PIECES], g_s[:, :], ssq[:, :], start=True, stop=True)
                elif kind == "centres":
                    pe.wait_ge(s_pooled.sem, s_pooled.at(own, 1))
                    for m in range(2):
                        for t in range(2):
                            mm(ps[:, 16 * m:16 * m + 16], wq[0:KP[t], t, 0, 128 * m:128 * m + 128],
                               pooled[0:KP[t], t, :], start=(t == 0), stop=(t == 1))
                    mm_t(ps[0:16, 64:64 + HC + 1], pooled[0:HC + 1, 0, :], id_s[0:HC + 1, 0:HC + 1])
                    last = mm_t(ps[0:16, 64 + HC + 1:64 + C + 1], pooled[0:HC, 1, :], id_s[0:HC, 0:HC])
                elif kind == "norms":
                    pe.wait_ge(s_csq.sem, s_csq.at(own, 1))
                    last = mm(ps[:, 0:32], hsum_s[:, :], csq[:, :], start=True, stop=True)
                elif kind == "pixels":
                    pe.wait_ge(s_cbd.sem, s_cbd.at(own, 1))
                    for t in range(2):
                        for m in range(2):
                            last = mm(ps[0:KP[t], 128 * t + 64 * m:128 * t + 64 * m + 64],
                                      w1n_s[:, m, (HC + 1) * t:(HC + 1) * t + KP[t]], cbd[:, m, :], start=True, stop=True)
                elif kind == "feat":
                    c, f = job[2:]
                    pe.wait_ge(s_xtok.sem, s_xtok.at(own, c + 1))
                    if c == 0 and f == 0:
                        wait_emptied(img, nxt, (1, "pixels"))
                    for t in range(2):
                        last = mm(ps[0:TOK, 0:D0 + HM], xtok[0:KP[t], c % 2, t, TOK * f:TOK * f + TOK], wq[0:KP[t], t, f, :],
                                  start=(t == 0), stop=(t == 1))
                elif kind == "tok":
                    c, h = job[2:]
                    for k in range(2):
                        o, q = (C + 1) * k, TOK * (2 * h + k)
                        mm_t(ps[0:TOK, o:o + HC + 1], xtok[0:HC + 1, c % 2, 0, q:q + TOK], id_s[0:HC + 1, 0:HC + 1])
                        last = mm_t(ps[0:TOK, o + HC + 1:o + C + 1], xtok[0:HC, c % 2, 1, q:q + TOK], id_s[0:HC, 0:HC])
                elif kind == "sums":
                    c = job[2]
                    pe.wait_ge(s_won.sem, s_won.at(own, c + 1))
                    wait_emptied(img, nxt, (1, "tok", c, 1))
                    if c == 0:
                        wait_emptied(img, nxt, (1, "centres"))
                        mm(ps[:, 0:C + 1], fsel_s[:, :], pooledT[:, :], start=True, stop=False, skip_group_check=True)
                    for f in range(4):
                        q = slice(HM * f, HM * f + HM)
                        mm(ps[q, 0:C + 1], won[:, q], xT[:, c % 2, f, :], start=(c > 0), stop=True, skip_group_check=True)
                    for f in range(4):
                        q = slice(HM * f, HM * f + HM)
                        mm(ps[q, C + 1:C + 2], key[:, q], ones[0:TOK, :], start=True, stop=True)
                    last = mm_t(ps[:, 256:256 + TOK], won[:, :], id_s[0:TOK, 0:TOK])
                elif kind == "sumsT":
                    pe.wait_ge(s_ys.sem, s_ys.at(own, 1))
                    mm_t(ps[0:HC + 1, 0:128], ys[:, 0:HC + 1], id_s[:, :])
                    last = mm_t(ps[0:HC, 128:256], ys[:, HC + 1:C + 1], id_s[:, :])
                elif kind == "agg":
                    wait_emptied(img, nxt, (1, "sumsT"))
                    for m in range(2):
                        for t in range(2):
                            last = mm(ps[:, 128 * m:128 * m + 128], wvt_s[0:KP[t], t, 128 * m:128 * m + 128],
                                      ysT[0:KP[t], t, :], start=(t == 0), stop=(t == 1))
                elif kind == "gout":
                    wait_emptied(img, nxt, (1, "agg"))
                    for m in range(2):
                        last = mm(ps[:, 0:C], agg[:, m, :], w2t_s[:, m, :], start=(m == 0), stop=(m == 1))
                elif kind == "out0":
                    wait_emptied(img, nxt, (1, "gout"))
                    t, hf, f = job[2] // 8, job[2] // 4 % 2, job[2] % 4
                    m = (4 if hf == 0 else 3) * TOK
                    q = slice(HM * f, HM * f + HM)
                    last = mm(ps[0:HC, 0:m], gout[q, HC * t:HC * t + HC], simT[q, 4 * TOK * hf:4 * TOK * hf + m],
                              start=True, stop=True)
                last.then_inc(s_job[turn].sem, 1)

            def turn(img, n, turns):
                nxt = img + 1 if 0 in turns else img
                for slot in range(SLOTS):
                    todo = [job for job in JOBS[slot] if job[0] in turns]
                    if 0 in turns and slot < STEPS:
                        if slot == 0:
                            for k in (1, 2):
                                job = (1, "qk", 1, k)
                                pe.wait_ge(s_emp[1, emptier(job)].sem, s_emp[1, emptier(job)].at(img, NTH_BY[job]))
                        elif slot % DUOS == 0:
                            b = slot // DUOS
                            if 2 <= b + 1 < NBAND:
                                for k in (1, 2):
                                    wait_emptied(img, nxt, (0, "qk", b + 1, k))
                        if slot >= 2:
                            pe.wait_ge(s_max.sem, s_max.at(img, slot - 1))
                        for j, (b, c, pair) in enumerate(units(slot)):
                            half, p0 = pair // 2, 64 * (pair % 2)
                            keys = rows(kpad[p0:p0 + 64, half, :], WP)[:, QB * b:QB * b + KB, QB * c:QB * c + KB]
                            last = mm(psS[slot % 2][:, j * NK:(j + 1) * NK], qbd[p0:p0 + 64, b % 3, half, c, :], keys,
                                      start=True, stop=True)
                        last.then_inc(s_scores.sem, 1)
                    first = 2 if all(job[1] == "out0" for job in todo[0:2]) else 1
                    for job in todo[0:first]:
                        fill(img, nxt, job, turns)
                    d = slot - 2
                    if 0 in turns and 0 <= d < STEPS:
                        pe.wait_ge(s_norm.sem, s_norm.at(img, d + 1))
                        if d >= 2:
                            pe.wait_ge(s_trs.sem, s_trs.at(img, d - 1))
                        for j in range(len(units(d))):
                            for k in range(2):
                                last = mm_t(psT[d % 2][0:KA, 256 * j + 128 * k:256 * j + 128 * k + 128],
                                            prob[:, d % 3, j, KA * k:KA * k + KA], id_s[:, :])
                        last.then_inc(s_tr.sem, 1)
                    for job in todo[first:2]:
                        fill(img, nxt, job, turns)
                    for d in (slot - 4, slot - 3) if 0 in turns and slot % 2 == 0 else ():
                        if not 0 <= d < STEPS:
                            continue
                        pe.wait_ge(s_trs.sem, s_trs.at(img, d + 1))
                        if d % DUOS == 0:
                            pe.wait_ge(s_vload.sem, s_vload.at(img, 16 * VLOADS * (d // DUOS + 2)))
                        for j, (b, c, pair) in enumerate(units(d)):
                            g = PAIRS * b + ORDER.index(pair)
                            if c == 0 and g >= 2:
                                pe.wait_ge(s_on.sem, s_on.at(img, g - 1))
                            for k, p in enumerate((KA, KBB)):
                                for e in range(2):
                                    q = slice(OROW[pair] + DH * e, OROW[pair] + DH * e + DH)
                                    o = 256 * j + 128 * k + 64 * e
                                    last = mm(psO[g % 2][q, 64 * c:64 * c + 64],
                                              vring[0:p, (b + k) % 3, c, VW * pair + DH * e:VW * pair + DH * e + DH],
                                              probT[0:p, d % 3, o:o + 64], start=(k == 0), stop=(k == 1), skip_group_check=True)
                            if c == NBAND - 1:
                                last.then_inc(s_av.sem, 1)
                    for job in todo[2:]:
                        fill(img, nxt, job, turns)

            images(pe, turn)


def kernel(x, L0_conv_W1, L0_conv_b1, L0_conv_Wv, L0_conv_bv, L0_conv_W2, L0_conv_b2, L0_conv_alpha, L0_conv_beta,
           L1_conv_qkv_w, L1_conv_qkv_b, L1_conv_proj_w, L1_conv_proj_b, L1_conv_bias_table):
    import numpy as np
    import concourse.bacc as bacc
    from concourse.bass_utils import run_bass_kernel_spmd

    def halves(wt):
        return np.ascontiguousarray(np.asarray(wt).reshape(2, HC, -1).transpose(1, 0, 2))

    def with_bias(wt, b):
        wt, b = np.asarray(wt), np.asarray(b)
        return np.concatenate([wt[:HC], b[None, :], wt[HC:]], 0)

    W1, W2, Wv, qkv, proj = (np.asarray(a) for a in (L0_conv_W1, L0_conv_W2, L0_conv_Wv, L1_conv_qkv_w, L1_conv_proj_w))
    qkv_b = np.asarray(L1_conv_qkv_b)
    w1n = np.concatenate([W1[:, :HC], np.asarray(L0_conv_b1)[:, None], W1[:, HC:]], 1)
    f = np.float32
    p = np.arange(128)
    chan = np.arange(HC)
    gmat = ((chan[:, None] // GC) == (chan[None, :] // GC)).astype(f) / f(GC * NPIX)
    hsum = ((p[:, None] // 32) == (p[None, :] // 32)).astype(f)
    fhm = np.arange(128)
    hmask = np.stack([((4 * m + p[:, None] // 32) == ((fhm % 32) // 4)[None, :]).astype(f) for m in range(2)], 1)
    rc = np.arange(16)
    R, Cc = rc // 4, rc % 4
    fold, cen = 2 * (R // 2) + Cc // 2, 2 * (R % 2) + Cc % 2
    fsel = ((fold[:, None] == (fhm // 32)[None, :]) & (cen[:, None] == (fhm % 4)[None, :])).astype(f)
    cmask = ((p[:, None] // 32) == (np.arange(16) // 4)[None, :]).astype(f)
    tie = np.broadcast_to(np.array([4, 3, 2, 1], f), (TOK, 4))
    qscale = np.stack([((p // 32) % 2 == e).astype(f) * f(DH ** -0.5) for e in range(2)], 1)
    arrays = {
        "x": np.asarray(x).reshape(B, C, NPIX),
        "w1t": with_bias(W1.T, L0_conv_b1), "w1n": w1n.reshape(2, 128, C + 1).transpose(1, 0, 2),
        "wvt": with_bias(Wv.T, L0_conv_bv), "w2t": W2.T.reshape(2, 128, C).transpose(1, 0, 2),
        "b2": np.asarray(L0_conv_b2).reshape(2, HC).T,
        "alpha": np.asarray(L0_conv_alpha).reshape(1, 1), "beta": np.asarray(L0_conv_beta).reshape(1, 1),
        "qk": halves(np.concatenate([qkv[:128], qkv[C:C + 128], qkv[128:C], qkv[C + 128:2 * C]], 0).T), "qb": qkv_b[:C, None], "kb": qkv_b[C:2 * C, None],
        "vt": with_bias(qkv[2 * C:].T, qkv_b[2 * C:]), "pt": proj.T,
        "pb": np.asarray(L1_conv_proj_b).reshape(2, HC).T, "table": np.asarray(L1_conv_bias_table).T,
        "ident": np.eye(128, dtype=f), "gmat": gmat, "hsum": hsum, "hmask": hmask, "fsel": fsel,
        "cmask": cmask, "tie": tie, "qscale": qscale,
    }
    nc = bacc.Bacc("TRN2", target_bir_lowering=False, num_devices=1)
    ins = {}
    arrays = {f"in_{k}": np.ascontiguousarray(v) for k, v in arrays.items()}
    for k, v in arrays.items():
        ins[k[3:]] = nc.dram_tensor(k, v.shape, mybir.dt.from_np(v.dtype), kind="ExternalInput").ap()
    out = nc.dram_tensor("out_0", (B, C, NPIX), F32, kind="ExternalOutput").ap()
    scratch = nc.dram_tensor("mask_scratch", (128 * PAIRS * NK,), F32, kind="Internal").ap()
    vmap = nc.dram_tensor("value_map", (HP * WP * PAIRS * VW,), F32, kind="Internal").ap()
    build(nc, out=out, scratch=scratch, vmap=vmap, **ins)
    r = run_bass_kernel_spmd(nc, [arrays], core_ids=[0])
    return r.results[0]["out_0"].reshape(B, C, H, W)
```
